# Optimizing a Trainium2 kernel written in Bass

```python
import numpy as np
import jax
import jax.numpy as jnp

def _softmax(x, axis=-1):
    return jax.nn.softmax(x, axis=axis)

def _gelu(x):
    return jax.nn.gelu(x, approximate=True)

def _silu(x):
    return jax.nn.silu(x)

def _sigmoid(x):
    return jax.nn.sigmoid(x)

def _layernorm(x, axis=-1, eps=1e-05):
    m = jnp.mean(x, axis=axis, keepdims=True)
    v = jnp.var(x, axis=axis, keepdims=True)
    return (x - m) / jnp.sqrt(v + eps)

def _scatter_add(tgt, idx, src, axis=0):
    return tgt.at[idx].add(src)

def _segment_sum(src, seg, n):
    return jax.ops.segment_sum(src, seg, n)
kernel_name = 'mk_seq_postln_d1_jaxref_r8_c81600'

def setup_inputs(seed: int=0):
    np.random.seed(seed)
    _w = jnp.asarray

    def _L0_attn_setup():
        import jax, jax.numpy as jnp
        import numpy as np
        B, N = (2, 256)
        H, R = (8, 64)
        IN_DIM, OUT_DIM = (64, 64)
        D = IN_DIM + OUT_DIM
        INIT = 1.0
        key = jax.random.key(seed)
        k1, k2, k3, k4 = jax.random.split(key, 4)
        x = jax.random.normal(k1, (B, N, D), dtype=jnp.float32)
        Wq = jax.random.normal(k2, (H * R, D), dtype=jnp.float32) * (INIT / np.sqrt(H * R * D))
        Wk = jax.random.normal(k3, (H * R, D), dtype=jnp.float32) * (INIT / np.sqrt(H * R * D))
        Wv = jax.random.normal(k4, (H * D, D), dtype=jnp.float32) * (INIT / np.sqrt(H * D * D))
        Wk = Wk.at[:, -1].set(0.0)
        rows = np.arange(1, H + 1) * D - 1
        Wv = Wv.at[rows, :IN_DIM].set(0.0)
        return {'x': x, 'Wq': Wq, 'Wk': Wk, 'Wv': Wv}
    _L0_attn_in = _L0_attn_setup()

    def _L0_ffn_setup():
        import jax, jax.numpy as jnp
        import numpy as np
        D_IN, D_HID = (128, 512)

        def _ternary(key, shape):
            return jax.random.randint(key, shape, -1, 2).astype(jnp.float32)

        def _tlin(x, w, s):
            return jnp.einsum('bsi,oi->bso', x, w) * s
        key = jax.random.key(seed)
        ks = jax.random.split(key, 12)
        inv = lambda fan: 1.0 / np.sqrt(fan).astype(np.float32)
        return {'x': jax.random.normal(ks[0], (4, 256, D_IN), dtype=jnp.float32), 'w1_w': _ternary(ks[1], (D_HID, D_IN)), 'w1_s': jax.random.uniform(ks[2], (D_HID,), dtype=jnp.float32) * inv(D_IN), 'w2_w': _ternary(ks[3], (D_HID, D_IN)), 'w2_s': jax.random.uniform(ks[4], (D_HID,), dtype=jnp.float32) * inv(D_IN), 'h1_w': _ternary(ks[5], (D_HID, D_HID)), 'h1_s': jax.random.uniform(ks[6], (D_HID,), dtype=jnp.float32) * inv(D_HID), 'h2_w': _ternary(ks[7], (D_HID, D_HID)), 'h2_s': jax.random.uniform(ks[8], (D_HID,), dtype=jnp.float32) * inv(D_HID), 'w3_w': _ternary(ks[9], (D_IN, D_HID)), 'w3_s': jax.random.uniform(ks[10], (D_IN,), dtype=jnp.float32) * inv(D_HID)}
    _L0_ffn_in = _L0_ffn_setup()
    _d = {'L0_attn_x': _L0_attn_in['x'], 'L0_attn_Wq': _L0_attn_in['Wq'], 'L0_attn_Wk': _L0_attn_in['Wk'], 'L0_attn_Wv': _L0_attn_in['Wv'], 'L0_ffn_w1_w': _L0_ffn_in['w1_w'], 'L0_ffn_w1_s': _L0_ffn_in['w1_s'], 'L0_ffn_w2_w': _L0_ffn_in['w2_w'], 'L0_ffn_w2_s': _L0_ffn_in['w2_s'], 'L0_ffn_h1_w': _L0_ffn_in['h1_w'], 'L0_ffn_h1_s': _L0_ffn_in['h1_s'], 'L0_ffn_h2_w': _L0_ffn_in['h2_w'], 'L0_ffn_h2_s': _L0_ffn_in['h2_s'], 'L0_ffn_w3_w': _L0_ffn_in['w3_w'], 'L0_ffn_w3_s': _L0_ffn_in['w3_s']}
    _x0 = _d['L0_attn_x']
    _d['L0_attn_x'] = jax.random.normal(jax.random.fold_in(jax.random.key(seed), 1), (32, 256, 128), dtype=_x0.dtype)
    del _x0
    return _d

def reference(L0_attn_x, L0_attn_Wq, L0_attn_Wk, L0_attn_Wv, L0_ffn_w1_w, L0_ffn_w1_s, L0_ffn_w2_w, L0_ffn_w2_s, L0_ffn_h1_w, L0_ffn_h1_s, L0_ffn_h2_w, L0_ffn_h2_s, L0_ffn_w3_w, L0_ffn_w3_s):

    def _L0_attn_ref(x, Wq, Wk, Wv):
        import jax, jax.numpy as jnp
        import numpy as np
        B, N = (2, 256)
        H, R = (8, 64)
        IN_DIM, OUT_DIM = (64, 64)
        D = IN_DIM + OUT_DIM
        INIT = 1.0
        b, n, d = x.shape
        Q = (x @ Wq.T).reshape(b, n, H, R)
        K = (x @ Wk.T).reshape(b, n, H, R)
        V = (x @ Wv.T).reshape(b, n, H, d)
        attn = jnp.einsum('bnhr,bmhr->bhnm', Q, K)
        attn = jax.nn.softmax(attn, axis=-1)
        out = jnp.einsum('bhnm,bmhd->bnd', attn, V)
        return out

    def _L0_ffn_ref(x, w1_w, w1_s, w2_w, w2_s, h1_w, h1_s, h2_w, h2_s, w3_w, w3_s):
        import jax, jax.numpy as jnp
        import numpy as np
        D_IN, D_HID = (128, 512)

        def _ternary(key, shape):
            return jax.random.randint(key, shape, -1, 2).astype(jnp.float32)

        def _tlin(x, w, s):
            return jnp.einsum('bsi,oi->bso', x, w) * s
        h = jax.nn.silu(_tlin(x, w1_w, w1_s)) * _tlin(x, w2_w, w2_s)
        h = jax.nn.gelu(_tlin(h, h1_w, h1_s), approximate=False)
        h = jax.nn.gelu(_tlin(h, h2_w, h2_s), approximate=False)
        return _tlin(h, w3_w, w3_s)
    x = L0_attn_x
    x = _layernorm(x + _L0_attn_ref(x, L0_attn_Wq, L0_attn_Wk, L0_attn_Wv), axis=-1)
    x = _layernorm(x + _L0_ffn_ref(x, L0_ffn_w1_w, L0_ffn_w1_s, L0_ffn_w2_w, L0_ffn_w2_s, L0_ffn_h1_w, L0_ffn_h1_s, L0_ffn_h2_w, L0_ffn_h2_s, L0_ffn_w3_w, L0_ffn_w3_s), axis=-1)
    return x

_drawn_inputs = setup_inputs


def setup_inputs(seed=0):
    import zlib

    import numpy as np

    out = dict(_drawn_inputs(seed))
    spreads = {}
    factors = {'L0_attn_Wq': 8.0,
     'L0_attn_Wk': 8.0,
     'L0_attn_Wv': 8.0,
     'L0_ffn_w1_w': 8.0,
     'L0_ffn_w1_s': 8.0,
     'L0_ffn_w2_w': 8.0,
     'L0_ffn_w2_s': 8.0,
     'L0_ffn_h1_w': 8.0,
     'L0_ffn_h1_s': 8.0,
     'L0_ffn_h2_w': 8.0,
     'L0_ffn_h2_s': 8.0,
     'L0_ffn_w3_w': 8.0,
     'L0_ffn_w3_s': 8.0}
    for name, (base, spread) in spreads.items():
        noise = np.random.default_rng([zlib.crc32(name.encode()), seed]).standard_normal(out[name].shape)
        drawn = base * np.exp(spread * noise) if base else spread * noise
        out[name] = jnp.asarray(drawn.astype(out[name].dtype))
    for name, factor in factors.items():
        out[name] = (out[name] * factor).astype(out[name].dtype)
    return out
```

```python
from contextlib import ExitStack

import concourse.bass as bass
from concourse import mybir

F32 = mybir.dt.float32
F32R = mybir.dt.float32r
I32 = mybir.dt.int32
ACT = mybir.ActivationFunctionType
ALU = mybir.AluOpType
AX = mybir.AxisListType

P = 128
D = 128
HID = 512
KC = HID // P
EPS = 1e-5
LEAD = 2
RING = 3
L1_SLOT, L2_SLOT, L3_SLOT, L4_SLOT = 2, 6, 10, 13
AT0_SLOT = 12


def layer_kernel(nc, x, wq, wk, wv, w1_w, w1_s, w2_w, w2_s, h1_w, h1_s, h2_w, h2_s, w3_w, w3_s, out):
    B, N, _ = x.shape
    H = wv.shape[0] // D
    R = wq.shape[0] // H
    PAIRS = B // 2
    TOK = 2 * N
    TT = TOK // P
    NT = N // P
    J = 2 * H
    VT = TT * H * D // TOK

    x_rows = x.rearrange("(i b) (t p) d -> i p (b t) d", b=2, p=P)
    out_rows = out.rearrange("(i b) (t p) d -> i p (b t) d", b=2, p=P)

    with ExitStack() as ctx:
        def sb(name, shape, dt=F32, at=None):
            return (at or ctx).enter_context(nc.sbuf_tensor(name, shape, dt))

        def sem(name):
            return ctx.enter_context(nc.semaphore(name))

        ident = sb("ident", [P, P])
        minus_half = sb("minus_half", [P, TT])
        NSC = 4 * KC + 2
        scales = sb("scales", [P, NSC])
        lo_max = sb("lo_max", [P, 8])
        lo_flag = sb("lo_flag", [P, 4])
        a_hi, a_lo = (sb(f"a_{s}", [P, H, D], F32R) for s in ("hi", "lo"))
        wv_hi, wv_lo = (sb(f"wv_{s}", [P, H * D], F32R) for s in ("hi", "lo"))
        w1_hi, w1_lo = (sb(f"w1_{s}", [P, HID], F32R) for s in ("hi", "lo"))
        w2_hi, w2_lo = (sb(f"w2_{s}", [P, HID], F32R) for s in ("hi", "lo"))
        h1_hi, h1_lo = (sb(f"h1_{s}", [P, KC, HID], F32R) for s in ("hi", "lo"))
        h2_hi, h2_lo = (sb(f"h2_{s}", [P, KC, HID], F32R) for s in ("hi", "lo"))
        w3_hi, w3_lo = (sb(f"w3_{s}", [P, KC, D], F32R) for s in ("hi", "lo"))

        with ExitStack() as early:
            wq_in = sb("wq_in", [R, H, D], at=early)
            wk_in = sb("wk_in", [R, H, D], at=early)
            wv_in = sb("wv_in", [P, H, D], at=early)
            w1_in = sb("w1_in", [P, KC, D], at=early)
            w2_in = sb("w2_in", [P, KC, D], at=early)
            h1_in = sb("h1_in", [P, KC, HID], at=early)
            h2_in = sb("h2_in", [P, KC, HID], at=early)
            w3_in = sb("w3_in", [P, HID], at=early)
            scales_in = sb("scales_in", [NSC, P], at=early)

        t_hi, t_lo = (sb(f"t_{s}", [P, H, TOK], F32R) for s in ("hi", "lo"))
        v_hi, v_lo = (sb(f"v_{s}", [P, TT, H * D], F32R) for s in ("hi", "lo"))
        prob = sb("prob", [P, RING, NT, N])
        pt_hi, pt_lo = (sb(f"pt_{s}", [P, RING, NT, N], F32R) for s in ("hi", "lo"))
        neg_max = sb("neg_max", [P, RING, NT])
        total = sb("total", [P, RING, NT])
        inv_total = sb("inv_total", [P, RING, NT])
        x_in = sb("x_in", [P, TT, D])
        res = sb("res", [P, TT, D])
        xt_hi, xt_lo = (sb(f"xt_{s}", [P, TOK], F32R) for s in ("hi", "lo"))
        at = sb("at", [P, N])
        x1 = sb("x1", [P, TT, D])
        x1t_hi, x1t_lo = (sb(f"x1t_{s}", [P, TOK], F32R) for s in ("hi", "lo"))
        silu_out = sb("silu_out", [P, 2, TOK])
        act32 = sb("act32", [P, RING, TOK])
        odd_hi, odd_lo = (sb(f"odd_{s}", [P, KC, TOK], F32R) for s in ("hi", "lo"))
        even_hi, even_lo = (sb(f"even_{s}", [P, KC, TOK], F32R) for s in ("hi", "lo"))
        yt = sb("yt", [P, TOK])
        y = sb("y", [P, TT, D])
        stats1, stats2 = (sb(f"stats{n}", [P, TT, 6]) for n in (1, 2))
        mv1, mv2 = (sb(f"mv{n}", [P, TT, 2]) for n in (1, 2))
        var_eps1, var_eps2 = (sb(f"var_eps{n}", [P, TT]) for n in (1, 2))
        rstd1, rstd2 = (sb(f"rstd{n}", [P, TT]) for n in (1, 2))

        bank = [ctx.enter_context(nc.psum_tensor(f"bank{n}", [P, 512], F32)) for n in range(8)]
        gp = bank[0:3]
        sc = bank[3:5]
        pt = bank[5:7]
        acc = bank[7]
        T_BANK = [gp[0], gp[1], sc[0], sc[1], gp[2], pt[0], gp[0], gp[1]]
        V_BANK = [pt[1], pt[0], gp[0], gp[1]] * 2
        AT_BANK = [gp[2], gp[2]]
        L1_BANK = [gp[n % 3] for n in range(2 * KC)]
        L2_BANK = [gp[2], gp[0], gp[1], gp[2]]
        L3_BANK = [gp[0], gp[1], gp[2], gp[0]]
        L4_BANK, YT_BANK, XT_BANK, X1T_BANK = gp[1], gp[0], gp[1], gp[2]

        (s_wqk, s_wv, s_wf, s_ident, s_prep_mm, s_prep_hi, s_prep_lo, s_lomax, s_flagt, s_flag,
         s_zero, s_scales_mm, s_scales, s_held) = (sem(n) for n in (
            "wqk_in", "wv_in", "wf_in", "ident_made", "prep_mm", "prep_hi", "prep_lo", "lomax_made",
            "flag_turned", "flag_made", "zeroed", "scales_mm", "scales_ready", "held"))
        s_xin, s_res, s_yfree = sem("x_in_landed"), sem("res_landed"), sem("y_free")
        s_xt_mm, s_xt_hi, s_xt_lo = sem("xt_mm"), sem("xt_hi"), sem("xt_lo")
        s_t_mm, s_t_hi, s_t_lo = sem("t_mm"), sem("t_hi"), sem("t_lo")
        s_v_mm, s_v_hi, s_v_lo = sem("v_mm"), sem("v_hi"), sem("v_lo")
        s_sc, s_max, s_exp, s_inv, s_norm = (sem(n) for n in ("scores", "max", "exp", "inv", "norm"))
        s_pt_mm, s_pt_hi, s_pt_lo, s_pv = (sem(n) for n in ("pt_mm", "pt_hi", "pt_lo", "pv"))
        s_acc, s_at, s_radd = sem("acc_copied"), sem("at_mm"), sem("res_added")
        s_ve1, s_rs1, s_x1 = sem("var_eps1"), sem("rstd1"), sem("x1_ready")
        s_st1, s_mv1, s_st2, s_mv2 = sem("stats1"), sem("mv1"), sem("stats2"), sem("mv2")
        s_x1t_mm, s_x1t_hi, s_x1t_lo = sem("x1t_mm"), sem("x1t_hi"), sem("x1t_lo")
        s_z1, s_z2, s_silu, s_gate = sem("z1"), sem("z2"), sem("silu"), sem("gate")
        s_l2, s_g2, s_l3, s_g3 = sem("l2_mm"), sem("gelu2"), sem("l3_mm"), sem("gelu3")
        s_1hi, s_1lo, s_2hi, s_2lo, s_3hi, s_3lo = (
            sem(f"l{n}_{s}") for n in (1, 2, 3) for s in ("hi", "lo"))
        s_l4, s_yt, s_yt_mm, s_yadd = sem("l4_mm"), sem("yt_ready"), sem("yt_mm"), sem("y_added")
        s_ve2, s_rs2, s_y = sem("var_eps2"), sem("rstd2"), sem("y_ready")

        block = ctx.enter_context(nc.Block())

        def steps(eng, step):
            step(0, None, False)
            with eng.Fori(1, PAIRS - 1) as i:
                step(i, i - 1, False)
            step(PAIRS - 1, PAIRS - 2, True)
            step(None, PAIRS - 1, True)

        G_FFN = 4
        PREP = [(a_hi[:, 0:4, :], a_lo[:, 0:4, :]), (a_hi[:, 4:8, :], a_lo[:, 4:8, :]),
                (wv_hi[:, 0:512], wv_lo[:, 0:512]), (wv_hi[:, 512:1024], wv_lo[:, 512:1024]),
                (w1_hi[:, :], w1_lo[:, :]), (w2_hi[:, :], w2_lo[:, :])]
        PREP += [(h1_hi[:, c, :], h1_lo[:, c, :]) for c in range(KC)]
        PREP += [(h2_hi[:, c, :], h2_lo[:, c, :]) for c in range(KC)]
        PREP += [(w3_hi[:, :, :], w3_lo[:, :, :])]
        NPREP = len(PREP)

        def hold(eng, s, value):
            eng.wait_ge(s, value)
            eng.sem_inc(s_held)

        def prep_bank(g, like):
            b = bank[g % 8][:, :]
            return b.rearrange("p (c n) -> p c n", n=D) if len(like.shape) == 3 else b

        @block.sync
        def _(sp):
            sp.dma_start(x_in[:, :, :], x_rows[0]).then_inc(s_xin, 16)
            sp.dma_start(wq_in[:, :, :], wq.rearrange("(h r) d -> r h d", h=H)).then_inc(s_wqk, 16)
            sp.dma_start(wk_in[:, :, :], wk.rearrange("(h r) d -> r h d", h=H)).then_inc(s_wqk, 16)
            sp.dma_start(wv_in[:, :, :], wv.rearrange("(h p) d -> p h d", h=H)).then_inc(s_wv, 16)
            sp.dma_start(w1_in[:, :, :], w1_w.rearrange("(c p) d -> p c d", p=P)).then_inc(s_wf, 16)
            sp.dma_start(w2_in[:, :, :], w2_w.rearrange("(c p) d -> p c d", p=P)).then_inc(s_wf, 16)
            sp.dma_start(h1_in[:, :, :], h1_w.rearrange("(c p) d -> p c d", p=P)).then_inc(s_wf, 16)
            sp.dma_start(h2_in[:, :, :], h2_w.rearrange("(c p) d -> p c d", p=P)).then_inc(s_wf, 16)
            sp.dma_start(w3_in[:, :], w3_w).then_inc(s_wf, 16)
            for n, s in enumerate((w1_s, w2_s, h1_s, h2_s)):
                sp.dma_start(scales_in[n * KC:(n + 1) * KC, :], s.rearrange("(c p) -> c p", p=P)).then_inc(s_wf, 16)
            for n in (4 * KC, 4 * KC + 1):
                sp.dma_start(scales_in[n:n + 1, :], w3_s.rearrange("(a p) -> a p", a=1)).then_inc(s_wf, 16)
            sp.dma_start(res[:, :, :], x_rows[0]).then_inc(s_res, 16)

            def step(i, f, last):
                if i is not None and not last:
                    sp.wait_ge(s_xt_mm, i + 1)
                    sp.dma_start(x_in[:, :, :], x_rows[i + 1]).then_inc(s_xin, 16)
                if f is not None:
                    if i is not None:
                        sp.wait_ge(s_x1, 2 * f + 2)
                        sp.dma_start(res[:, :, :], x_rows[i]).then_inc(s_res, 16)
                    sp.wait_ge(s_y, f + 1)
                    sp.dma_start(out_rows[f], y[:, :, :]).then_inc(s_yfree, 16)

            steps(sp, step)
            sp.wait_ge(s_yfree, 16 * (PAIRS + 1))

        @block.gpsimd
        def _(pool):
            nc.gpsimd.memset(ident[:, :], 0.0).then_inc(s_zero, 1)
            nc.gpsimd.memset(minus_half[:, :], -0.5).then_inc(s_zero, 1)
            nc.gpsimd.memset(y[:, :, :], 0.0).then_inc(s_yfree, 16)
            pool.wait_ge(s_zero, 1)
            nc.gpsimd.affine_select(out=ident[:, :], in_=ident[:, :], compare_op=ALU.not_equal, fill=1.0,
                                    base=0, pattern=[[-1, P]], channel_multiplier=1).then_inc(s_ident, 1)

            def norm(i, j):
                hold(pool, s_inv, i * J + j + 1)
                for nt in range(NT):
                    last = nc.gpsimd.tensor_scalar(prob[:, j % RING, nt, :], prob[:, j % RING, nt, :],
                                                   inv_total[:, j % RING, nt:nt + 1], None, ALU.mult)
                last.then_inc(s_norm, 1)

            def split(f, c, hi, lo, s_in, s_hi, s_lo):
                hold(pool, s_in, f * KC + c + 1)
                nc.gpsimd.tensor_copy(hi[:, c, :], act32[:, c % RING, :]).then_inc(s_hi, 1)
                if lo is not None:
                    pool.wait_ge(s_hi, f * KC + c + 1)
                    nc.gpsimd.tensor_tensor(lo[:, c, :], act32[:, c % RING, :], hi[:, c, :].bitcast(F32),
                                            ALU.subtract).then_inc(s_lo, 1)

            def layer_norm(count, first, n, src, dst, mv, var_eps, rstd, s_mv, s_ve, s_rs, s_out):
                tiles = slice(first, first + n)
                hold(pool, s_mv, (count + 1) * n)
                nc.gpsimd.tensor_scalar(var_eps[:, tiles], mv[:, tiles, 1], EPS, None,
                                        ALU.add).then_inc(s_ve, 1)
                pool.wait_ge(s_ve, count + 1)
                nc.gpsimd.tensor_tensor(rstd[:, tiles], var_eps[:, tiles], minus_half[:, tiles],
                                        ALU.pow).then_inc(s_rs, 1)
                hold(pool, s_rs, count + 1)
                for t in range(first, first + n):
                    last = nc.gpsimd.tensor_scalar(dst[:, t, :], src[:, t, :], mv[:, t, 0:1],
                                                   rstd[:, t:t + 1], ALU.subtract, ALU.mult)
                last.then_inc(s_out, 1)

            def norm1(f, b):
                layer_norm(2 * f + b, NT * b, NT, res, x1, mv1, var_eps1, rstd1, s_mv1, s_ve1, s_rs1, s_x1)

            def step(i, f, last):
                if f is not None:
                    norm1(f, 1)
                if i is not None:
                    for j in range(LEAD):
                        norm(i, j)
                for j in range(J):
                    if i is not None and j + LEAD < J:
                        norm(i, j + LEAD)
                    if f is not None:
                        if j == L1_SLOT:
                            for c in range(KC):
                                split(f, c, odd_hi, None, s_gate, s_1hi, None)
                        if j == L2_SLOT:
                            for c in range(KC):
                                split(f, c, even_hi, even_lo, s_g2, s_2hi, s_2lo)
                        if j == L3_SLOT:
                            for c in range(KC):
                                split(f, c, odd_hi, odd_lo, s_g3, s_3hi, s_3lo)
                if f is not None:
                    pool.wait_ge(s_yfree, 16 * (f + 1))
                    layer_norm(f, 0, TT, x1, y, mv2, var_eps2, rstd2, s_mv2, s_ve2, s_rs2, s_y)
                if i is not None:
                    norm1(i, 0)

            steps(pool, step)

        @block.scalar
        def _(act):
            def copy(dst, src):
                return nc.scalar.activation(dst, src, ACT.Copy)

            for g, (hi, _lo) in enumerate(PREP):
                act.wait_ge(s_prep_mm, g + 1)
                copy(hi, prep_bank(g, hi)).then_inc(s_prep_hi, 1)
            act.wait_ge(s_scales_mm, 1)
            copy(scales[:, :], acc[:, 0:NSC]).then_inc(s_scales, 1)
            act.wait_ge(s_scales, 1)

            def xt_part(i):
                act.wait_ge(s_xt_mm, i + 1)
                copy(xt_hi[:, :], XT_BANK[:, :]).then_inc(s_xt_hi, 1)

            def acc_copy(i, b):
                act.wait_ge(s_pv, i * J + (b + 1) * H)
                if b == 1:
                    act.wait_ge(s_at, 2 * i + 1)
                elif not isinstance(i, int) or i > 0:
                    act.wait_ge(s_at, 2 * i)
                copy(at[:, :], acc[:, b * N:(b + 1) * N]).then_inc(s_acc, 1)

            def exp(i, j):
                act.wait_ge(s_max, i * J + j + 1)
                if j >= RING:
                    act.wait_ge(s_pt_mm, i * J + j - RING + 1)
                for nt in range(NT):
                    last = nc.scalar.activation(prob[:, j % RING, nt, :], sc[j % 2][:, nt * N:(nt + 1) * N],
                                                ACT.Exp, bias=neg_max[:, j % RING, nt:nt + 1],
                                                accum_out=total[:, j % RING, nt:nt + 1])
                last.then_inc(s_exp, 1)

            def pt_part(i, j):
                act.wait_ge(s_pt_mm, i * J + j + 1)
                if j >= RING:
                    act.wait_ge(s_pv, i * J + j - RING + 1)
                copy(pt_hi[:, j % RING, :, :], pt[j % 2].rearrange("p (t n) -> p t n", n=N)).then_inc(s_pt_hi, 1)

            def v_part(i, v):
                act.wait_ge(s_v_mm, i * VT + v + 1)
                copy(v_hi[:, v // 2, (v % 2) * 512:(v % 2 + 1) * 512], V_BANK[v][:, :]).then_inc(s_v_hi, 1)

            def gelus(f, banks, n_scale, s_mm, s_out, s_lo):
                for c in range(KC):
                    act.wait_ge(s_mm, f * KC + c + 1)
                    if c >= RING:
                        act.wait_ge(s_lo, f * KC + c - RING + 1)
                    nc.scalar.activation(act32[:, c % RING, :], banks[c][:, :], ACT.Gelu,
                                         scale=scales[:, n_scale * KC + c:n_scale * KC + c + 1]).then_inc(s_out, 1)

            xt_part(0)

            def step(i, f, last):
                if f is not None:
                    acc_copy(f, 1)
                if i is not None:
                    for h in range(H):
                        act.wait_ge(s_t_mm, i * H + h + 1)
                        copy(t_hi[:, h, :], T_BANK[h][:, :]).then_inc(s_t_hi, 1)
                    for v in range(VT):
                        if v < LEAD:
                            exp(i, v)
                        v_part(i, v)
                for j in range(J):
                    if i is not None:
                        if j + LEAD < J:
                            exp(i, j + LEAD)
                        pt_part(i, j)
                    if j == 0 and f is not None:
                        act.wait_ge(s_x1t_mm, f + 1)
                        copy(x1t_hi[:, :], X1T_BANK[:, :]).then_inc(s_x1t_hi, 1)
                    if i is not None and j == H + 1:
                        acc_copy(i, 0)
                    if f is None:
                        continue
                    if j == L1_SLOT:
                        for c in range(KC):
                            act.wait_ge(s_z1, f * KC + c + 1)
                            if c >= 2:
                                act.wait_ge(s_gate, f * KC + c - 1)
                            nc.scalar.activation(silu_out[:, c % 2, :], L1_BANK[2 * c][:, :], ACT.Silu,
                                                 scale=scales[:, c:c + 1]).then_inc(s_silu, 1)
                    if j == L2_SLOT:
                        gelus(f, L2_BANK, 2, s_l2, s_g2, s_2lo)
                    if j == L3_SLOT:
                        gelus(f, L3_BANK, 3, s_l3, s_g3, s_3lo)
                    if j == L4_SLOT:
                        act.wait_ge(s_l4, f + 1)
                        nc.scalar.activation(yt[:, :], L4_BANK[:, :], ACT.Copy,
                                             scale=scales[:, 4 * KC:4 * KC + 1]).then_inc(s_yt, 1)
                if i is not None and not last:
                    xt_part(i + 1)

            steps(act, step)

        @block.vector
        def _(dve):
            def minus(dst, src, hi):
                return nc.vector.tensor_tensor(dst, src, hi.bitcast(F32), ALU.subtract)

            for g, (hi, lo) in enumerate(PREP):
                dve.wait_ge(s_prep_hi, g + 1)
                minus(lo, prep_bank(g, lo), hi).then_inc(s_prep_lo, 1)

            def xt_part(i):
                dve.wait_ge(s_xt_hi, i + 1)
                minus(xt_lo[:, :], XT_BANK[:, :], xt_hi[:, :]).then_inc(s_xt_lo, 1)

            def flag():
                dve.wait_ge(s_prep_lo, NPREP)
                for n, lo in enumerate((w1_lo[:, :], w2_lo[:, :], h1_lo[:, :, :], h2_lo[:, :, :], w3_lo[:, :, :])):
                    nc.vector.tensor_reduce(lo_max[:, n:n + 1], lo.bitcast(F32), AX.X if n < 2 else AX.XY,
                                            ALU.max, apply_absolute_value=True).then_inc(s_lomax, 1)
                dve.wait_ge(s_lomax, 5)
                nc.vector.tensor_reduce(lo_max[:, 5:6], lo_max[:, 0:5], AX.X, ALU.max).then_inc(s_lomax, 1)
                dve.wait_ge(s_flagt, 1)
                nc.vector.tensor_reduce(lo_flag[0:1, 0:1], acc[0:1, 0:P], AX.X, ALU.max).then_inc(s_flag, 1)

            def res_add(i, b):
                dve.wait_ge(s_at, 2 * i + b + 1)
                if b == 0:
                    dve.wait_ge(s_res, 16 * (i + 1))
                half = res[:, NT * b:NT * (b + 1), :]
                nc.vector.tensor_tensor(half, AT_BANK[b][:, 0:N].rearrange("p (t d) -> p t d", d=D), half,
                                        ALU.add).then_inc(s_radd, 1)
                dve.wait_ge(s_radd, 2 * i + b + 1)
                for t in range(NT * b, NT * (b + 1)):
                    nc.vector.bn_stats(stats1[:, t, :], res[:, t, :]).then_inc(s_st1, 1)
                for t in range(NT * b, NT * (b + 1)):
                    hold(dve, s_st1, i * TT + t + 1)
                    nc.vector.bn_aggr(mv1[:, t, :], stats1[:, t, :]).then_inc(s_mv1, 1)

            def row_max(i, j):
                dve.wait_ge(s_sc, i * J + j + 1)
                nc.vector.tensor_reduce(neg_max[:, j % RING, :], sc[j % 2].rearrange("p (t m) -> p t m", m=N),
                                        AX.X, ALU.max, negate=True).then_inc(s_max, 1)

            def inverse(i, j):
                dve.wait_ge(s_exp, i * J + j + 1)
                nc.vector.reciprocal(inv_total[:, j % RING, :], total[:, j % RING, :]).then_inc(s_inv, 1)

            def l1_lo(f, c):
                dve.wait_ge(s_1hi, f * KC + c + 1)
                minus(odd_lo[:, c, :], act32[:, c % RING, :], odd_hi[:, c, :]).then_inc(s_1lo, 1)

            xt_part(0)
            flag()

            def step(i, f, last):
                if i is not None:
                    for h in range(H):
                        dve.wait_ge(s_t_hi, i * H + h + 1)
                        minus(t_lo[:, h, :], T_BANK[h][:, :], t_hi[:, h, :]).then_inc(s_t_lo, 1)
                    for j in range(LEAD):
                        row_max(i, j)
                if f is not None:
                    res_add(f, 1)
                if i is not None:
                    for v in range(VT):
                        if v < LEAD:
                            inverse(i, v)
                        dve.wait_ge(s_v_hi, i * VT + v + 1)
                        cols = slice((v % 2) * 512, (v % 2 + 1) * 512)
                        minus(v_lo[:, v // 2, cols], V_BANK[v][:, :], v_hi[:, v // 2, cols]).then_inc(s_v_lo, 1)
                for j in range(J):
                    if i is not None:
                        if j + LEAD < J:
                            row_max(i, j + LEAD)
                            inverse(i, j + LEAD)
                        dve.wait_ge(s_pt_hi, i * J + j + 1)
                        minus(pt_lo[:, j % RING, :, :], pt[j % 2].rearrange("p (t n) -> p t n", n=N),
                              pt_hi[:, j % RING, :, :]).then_inc(s_pt_lo, 1)
                    if j == 0 and f is not None:
                        dve.wait_ge(s_x1t_hi, f + 1)
                        minus(x1t_lo[:, :], X1T_BANK[:, :], x1t_hi[:, :]).then_inc(s_x1t_lo, 1)
                    if j == AT0_SLOT and i is not None:
                        res_add(i, 0)
                    if j == L1_SLOT and f is not None:
                        for c in range(KC):
                            dve.wait_ge(s_silu, f * KC + c + 1)
                            dve.wait_ge(s_z2, f * KC + c + 1)
                            if c >= RING:
                                dve.wait_ge(s_1lo, f * KC + c - RING + 1)
                            nc.vector.scalar_tensor_tensor(
                                out=act32[:, c % RING, :], in0=L1_BANK[2 * c + 1][:, :], scalar=scales[:, KC + c:KC + c + 1],
                                in1=silu_out[:, c % 2, :], op0=ALU.mult, op1=ALU.mult).then_inc(s_gate, 1)
                            if c >= 1:
                                l1_lo(f, c - 1)
                        l1_lo(f, KC - 1)
                if f is not None:
                    dve.wait_ge(s_yt_mm, f + 1)
                    nc.vector.tensor_tensor(x1[:, :, :], YT_BANK.rearrange("p (t d) -> p t d", d=D), x1[:, :, :],
                                            ALU.add).then_inc(s_yadd, 1)
                if i is not None and not last:
                    xt_part(i + 1)
                if f is not None:
                    dve.wait_ge(s_yadd, f + 1)
                    for t in range(TT):
                        nc.vector.bn_stats(stats2[:, t, :], x1[:, t, :]).then_inc(s_st2, 1)
                    for t in range(TT):
                        hold(dve, s_st2, f * TT + t + 1)
                        nc.vector.bn_aggr(mv2[:, t, :], stats2[:, t, :]).then_inc(s_mv2, 1)

            steps(dve, step)

        @block.tensor
        def _(pe):
            mm, turn = nc.tensor.matmul, nc.tensor.transpose

            def three(dst, w_hi, w_lo, m_hi, m_lo, start, stop):
                mm(dst, w_hi, m_hi, start=start, stop=False)
                mm(dst, w_hi, m_lo, start=False, stop=False)
                return mm(dst, w_lo, m_hi, start=False, stop=stop)

            def turns(dst, blocks, s_out):
                for n, b in enumerate(blocks):
                    last = turn(dst[:, n * P:(n + 1) * P], b, ident[:, :])
                last.then_inc(s_out, 1)

            def turn_x(i):
                pe.wait_ge(s_xin, 16 * (i + 1))
                turns(XT_BANK, [x_in[:, t, :] for t in range(TT)], s_xt_mm)

            pe.wait_ge(s_wqk, 32)
            for g in range(2):
                for h in range(4):
                    last = mm(bank[g][:, h * D:(h + 1) * D], wq_in[:, 4 * g + h, :], wk_in[:, 4 * g + h, :],
                              start=True, stop=True)
                last.then_inc(s_prep_mm, 1)
            pe.wait_ge(s_ident, 1)
            pe.wait_ge(s_wv, 16)
            for g in range(2):
                turns(bank[2 + g], [wv_in[:, 4 * g + h, :] for h in range(4)], s_prep_mm)
            pe.wait_ge(s_wf, 16 * 11)
            blocks = [[w1_in[:, c, :] for c in range(KC)], [w2_in[:, c, :] for c in range(KC)]]
            for w in (h1_in, h2_in):
                blocks += [[w[:, o, c * P:(c + 1) * P] for o in range(KC)] for c in range(KC)]
            blocks += [[w3_in[:, c * P:(c + 1) * P] for c in range(KC)]]
            for n, b in enumerate(blocks):
                g = G_FFN + n
                if g >= 8:
                    pe.wait_ge(s_prep_lo, g - 7)
                turns(bank[g % 8], b, s_prep_mm)
            pe.wait_ge(s_prep_lo, NPREP)
            turn_x(0)
            turn(acc[:, 0:NSC], scales_in[:, :], ident[0:NSC, 0:NSC]).then_inc(s_scales_mm, 1)
            pe.wait_ge(s_scales, 1)
            pe.wait_ge(s_lomax, 6)
            turn(acc[0:1, 0:P], lo_max[:, 5:6], ident[:, :]).then_inc(s_flagt, 1)
            pe.wait_ge(s_flag, 1)
            any_lo = pe.value_load(lo_flag[0:1, 0:1].bitcast(I32))

            def layer(o, dst, w_hi, w_lo, m_hi, m_lo, s_parts, f, with_lo):
                n = len(w_hi)
                for c in range(n):
                    if s_parts is not None and o == 0:
                        pe.wait_ge(s_parts, f * KC + c + 1)
                    mm(dst, w_hi[c], m_hi[c], start=(c == 0), stop=False)
                    last = mm(dst, w_hi[c], m_lo[c], start=False, stop=(c == n - 1 and not with_lo))
                    if with_lo:
                        last = mm(dst, w_lo[c], m_hi[c], start=False, stop=(c == n - 1))
                return last

            def either(emit):
                with pe.If(any_lo):
                    emit(True)
                with pe.Else():
                    emit(False)

            def layer1(i, f, with_lo):
                for o in range(KC):
                    cols = slice(o * P, (o + 1) * P)
                    for which, (hi, lo, s_out) in enumerate(((w1_hi, w1_lo, s_z1), (w2_hi, w2_lo, s_z2))):
                        n = 2 * o + which
                        if n == 0:
                            pe.wait_ge(s_x1t_lo, f + 1)
                        if n in (0, 1) and i is not None:
                            pe.wait_ge(s_v_lo, i * VT + VT - 1 + n)
                        if n >= 3:
                            m = (n - 3) // 2
                            pe.wait_ge(s_gate if (n - 3) % 2 else s_silu, f * KC + m + 1)
                        layer(o, L1_BANK[n][:, :], [hi[:, cols]], [lo[:, cols]], [x1t_hi[:, :]],
                              [x1t_lo[:, :]], None, f, with_lo).then_inc(s_out, 1)

            def layer23(f, banks, w_hi, w_lo, m_hi, m_lo, s_prior, n_prior, s_parts, s_free, s_out, with_lo):
                pe.wait_ge(s_prior, f * KC + n_prior)
                for o in range(KC):
                    cols = slice(o * P, (o + 1) * P)
                    if o == KC - 1:
                        pe.wait_ge(s_free, f * KC + 1)
                    layer(o, banks[o][:, :], [w_hi[:, c, cols] for c in range(KC)],
                          [w_lo[:, c, cols] for c in range(KC)], [m_hi[:, c, :] for c in range(KC)],
                          [m_lo[:, c, :] for c in range(KC)], s_parts, f, with_lo).then_inc(s_out, 1)

            def layer4(f, with_lo):
                pe.wait_ge(s_g3, f * KC + 2)
                layer(0, L4_BANK[:, :], [w3_hi[:, c, :] for c in range(KC)], [w3_lo[:, c, :] for c in range(KC)],
                      [odd_hi[:, c, :] for c in range(KC)], [odd_lo[:, c, :] for c in range(KC)],
                      s_3lo, f, with_lo).then_inc(s_l4, 1)

            def project_t(i):
                pe.wait_ge(s_xt_lo, i + 1)
                for h in range(H):
                    if h >= 6:
                        pe.wait_ge(s_t_lo, i * H + h - 5)
                    three(T_BANK[h][:, :], a_hi[:, h, :], a_lo[:, h, :], xt_hi[:, :], xt_lo[:, :],
                          True, True).then_inc(s_t_mm, 1)

            def project_v(i):
                for v in range(VT):
                    if 1 <= v < 4:
                        pe.wait_ge(s_t_lo, i * H + 5 + v)
                    if v >= 4:
                        pe.wait_ge(s_v_lo, i * VT + v - 3)
                    rows = slice((v // 2) * P, (v // 2 + 1) * P)
                    cols = slice((v % 2) * 512, (v % 2 + 1) * 512)
                    three(V_BANK[v][:, :], xt_hi[:, rows], xt_lo[:, rows], wv_hi[:, cols], wv_lo[:, cols],
                          True, True).then_inc(s_v_mm, 1)

            def scores(i, j):
                b, h = j // H, j % H
                if j < H:
                    pe.wait_ge(s_t_lo, i * H + max(h + 1, j + 3 if j < 2 else 0))
                if j >= 2:
                    pe.wait_ge(s_exp, i * J + j - 1)
                for nt in range(NT):
                    q = slice(b * N + nt * P, b * N + (nt + 1) * P)
                    m = slice(b * N, (b + 1) * N)
                    last = three(sc[j % 2][:, nt * N:(nt + 1) * N], t_hi[:, h, q], t_lo[:, h, q],
                                 xt_hi[:, m], xt_lo[:, m], True, True)
                last.then_inc(s_sc, 1)

            def turn_prob(i, j):
                pe.wait_ge(s_norm, i * J + j + 1)
                if j < 2:
                    pe.wait_ge(s_v_lo, i * VT + 6 - j)
                else:
                    pe.wait_ge(s_pt_lo, i * J + j - 1)
                turns(pt[j % 2], [prob[:, j % RING, nt, mt * P:(mt + 1) * P]
                                  for mt in range(NT) for nt in range(NT)], s_pt_mm)

            def times_v(i, j):
                b, h = j // H, j % H
                pe.wait_ge(s_pt_lo, i * J + j + 1)
                if j == 0:
                    pe.wait_ge(s_v_lo, (i + 1) * VT)
                if j == H:
                    pe.wait_ge(s_acc, 2 * i + 1)
                for mt in range(NT):
                    v = slice(h * D, (h + 1) * D)
                    last = three(acc[:, b * N:(b + 1) * N], v_hi[:, b * NT + mt, v], v_lo[:, b * NT + mt, v],
                                 pt_hi[:, j % RING, mt, :], pt_lo[:, j % RING, mt, :],
                                 h == 0 and mt == 0, h == H - 1 and mt == NT - 1)
                last.then_inc(s_pv, 1)

            def turn_attention(i, b):
                pe.wait_ge(s_acc, 2 * i + b + 1)
                turns(AT_BANK[b], [at[:, t * P:(t + 1) * P] for t in range(NT)], s_at)

            def step(i, f, last):
                if i is not None:
                    project_t(i)
                if f is not None:
                    if i is not None:
                        pe.wait_ge(s_t_lo, i * H + 5)
                    turn_attention(f, 1)
                if i is not None:
                    for j in range(LEAD):
                        scores(i, j)
                    project_v(i)
                for j in range(J):
                    if i is not None:
                        if j + LEAD < J:
                            scores(i, j + LEAD)
                        turn_prob(i, j)
                        if j >= 2:
                            times_v(i, j - 2)
                    if f is not None:
                        if j == 0:
                            pe.wait_ge(s_x1, 2 * f + 2)
                            turns(X1T_BANK, [x1[:, t, :] for t in range(TT)], s_x1t_mm)
                        if j == L1_SLOT:
                            either(lambda w: layer1(i, f, w))
                        if j == L2_SLOT:
                            either(lambda w: layer23(f, L2_BANK, h1_hi, h1_lo, odd_hi, odd_lo, s_gate, 3, s_1lo, s_g2, s_l2, w))
                        if j == L3_SLOT:
                            either(lambda w: layer23(f, L3_BANK, h2_hi, h2_lo, even_hi, even_lo, s_g2, 2, s_2lo, s_g3, s_l3, w))
                        if j == L4_SLOT:
                            either(lambda w: layer4(f, w))
                    if j == AT0_SLOT and i is not None:
                        if f is not None:
                            pe.wait_ge(s_g3, f * KC + 3)
                        turn_attention(i, 0)
                if i is not None:
                    times_v(i, J - 2)
                if f is not None:
                    pe.wait_ge(s_yt, f + 1)
                    turns(YT_BANK, [yt[:, t * P:(t + 1) * P] for t in range(TT)], s_yt_mm)
                if i is not None:
                    if not last:
                        turn_x(i + 1)
                    times_v(i, J - 1)

            steps(pe, step)


_INS = ["L0_attn_x", "L0_attn_Wq", "L0_attn_Wk", "L0_attn_Wv", "L0_ffn_w1_w", "L0_ffn_w1_s", "L0_ffn_w2_w",
        "L0_ffn_w2_s", "L0_ffn_h1_w", "L0_ffn_h1_s", "L0_ffn_h2_w", "L0_ffn_h2_s", "L0_ffn_w3_w", "L0_ffn_w3_s"]


def kernel(**inputs):
    import numpy as np
    import concourse.bacc as bacc
    from concourse.bass_utils import run_bass_kernel_spmd

    nc = bacc.Bacc("TRN2", target_bir_lowering=False, num_devices=1)
    arrays, args = {}, []
    for name in _INS:
        a = np.ascontiguousarray(inputs[name])
        arrays[f"in_{name}"] = a
        args.append(nc.dram_tensor(f"in_{name}", a.shape, mybir.dt.from_np(a.dtype), kind="ExternalInput").ap())
    shape = arrays["in_L0_attn_x"].shape
    args.append(nc.dram_tensor("out_x", shape, F32, kind="ExternalOutput").ap())
    layer_kernel(nc, *args)
    r = run_bass_kernel_spmd(nc, [arrays], core_ids=[0])
    return r.results[0]["out_x"]
```

```python
from contextlib import ExitStack

import concourse.bass as bass
from concourse import mybir

F32 = mybir.dt.float32
F32R = mybir.dt.float32r
I32 = mybir.dt.int32
ACT = mybir.ActivationFunctionType
ALU = mybir.AluOpType
AX = mybir.AxisListType

P = 128
D = 128
HID = 512
KC = HID // P
EPS = 1e-5
LEAD = 3
PRING = 4
RING = 3
L1_SLOT, L2_SLOT, L3_SLOT, L4_SLOT = 2, 6, 10, 14
AT0_SLOT = 12


def layer_kernel(nc, x, wq, wk, wv, w1_w, w1_s, w2_w, w2_s, h1_w, h1_s, h2_w, h2_s, w3_w, w3_s, out):
    B, N, _ = x.shape
    H = wv.shape[0] // D
    R = wq.shape[0] // H
    PAIRS = B // 2
    TOK = 2 * N
    TT = TOK // P
    NT = N // P
    J = 2 * H
    VT = TT * H * D // TOK

    x_rows = x.rearrange("(i b) (t p) d -> i p (b t) d", b=2, p=P)
    out_rows = out.rearrange("(i b) (t p) d -> i p (b t) d", b=2, p=P)

    with ExitStack() as ctx:
        def sb(name, shape, dt=F32, at=None):
            return (at or ctx).enter_context(nc.sbuf_tensor(name, shape, dt))

        def sem(name):
            return ctx.enter_context(nc.semaphore(name))

        ident = sb("ident", [P, P])
        minus_half = sb("minus_half", [P, TT])
        NSC = 4 * KC + 2
        scales = sb("scales", [P, NSC])
        lo_max = sb("lo_max", [P, 8])
        lo_flag = sb("lo_flag", [P, 4])
        a_hi, a_lo = (sb(f"a_{s}", [P, H, D], F32R) for s in ("hi", "lo"))
        wv_hi, wv_lo = (sb(f"wv_{s}", [P, H * D], F32R) for s in ("hi", "lo"))
        w1_hi, w1_lo = (sb(f"w1_{s}", [P, HID], F32R) for s in ("hi", "lo"))
        w2_hi, w2_lo = (sb(f"w2_{s}", [P, HID], F32R) for s in ("hi", "lo"))
        h1_hi, h1_lo = (sb(f"h1_{s}", [P, KC, HID], F32R) for s in ("hi", "lo"))
        h2_hi, h2_lo = (sb(f"h2_{s}", [P, KC, HID], F32R) for s in ("hi", "lo"))
        w3_hi, w3_lo = (sb(f"w3_{s}", [P, KC, D], F32R) for s in ("hi", "lo"))

        with ExitStack() as early:
            wq_in = sb("wq_in", [R, H, D], at=early)
            wk_in = sb("wk_in", [R, H, D], at=early)
            wv_in = sb("wv_in", [P, H, D], at=early)
            w1_in = sb("w1_in", [P, KC, D], at=early)
            w2_in = sb("w2_in", [P, KC, D], at=early)
            h1_in = sb("h1_in", [P, KC, HID], at=early)
            h2_in = sb("h2_in", [P, KC, HID], at=early)
            w3_in = sb("w3_in", [P, HID], at=early)
            scales_in = sb("scales_in", [NSC, P], at=early)

        t_hi, t_lo = (sb(f"t_{s}", [P, H, TOK], F32R) for s in ("hi", "lo"))
        v_hi, v_lo = (sb(f"v_{s}", [P, TT, H * D], F32R) for s in ("hi", "lo"))
        prob = sb("prob", [P, PRING, NT, N])
        pt_hi, pt_lo = (sb(f"pt_{s}", [P, RING, NT, N], F32R) for s in ("hi", "lo"))
        neg_max = sb("neg_max", [P, PRING, NT])
        total = sb("total", [P, PRING, NT])
        inv_total = sb("inv_total", [P, PRING, NT])
        x_in = sb("x_in", [P, TT, D])
        res = sb("res", [P, TT, D])
        xt_hi, xt_lo = (sb(f"xt_{s}", [P, TOK], F32R) for s in ("hi", "lo"))
        at = sb("at", [P, N])
        x1 = sb("x1", [P, TT, D])
        x1t_hi, x1t_lo = (sb(f"x1t_{s}", [P, TOK], F32R) for s in ("hi", "lo"))
        silu_out = sb("silu_out", [P, 2, TOK])
        act32 = sb("act32", [P, RING, TOK])
        odd_hi, odd_lo = (sb(f"odd_{s}", [P, KC, TOK], F32R) for s in ("hi", "lo"))
        even_hi, even_lo = (sb(f"even_{s}", [P, KC, TOK], F32R) for s in ("hi", "lo"))
        yt = sb("yt", [P, TOK])
        y = sb("y", [P, TT, D])
        stats1, stats2 = (sb(f"stats{n}", [P, TT, 6]) for n in (1, 2))
        mv1, mv2 = (sb(f"mv{n}", [P, TT, 2]) for n in (1, 2))
        var_eps1, var_eps2 = (sb(f"var_eps{n}", [P, TT]) for n in (1, 2))
        rstd1, rstd2 = (sb(f"rstd{n}", [P, TT]) for n in (1, 2))

        bank = [ctx.enter_context(nc.psum_tensor(f"bank{n}", [P, 512], F32)) for n in range(8)]
        gp = bank[0:3]
        sc = bank[3:5]
        pt = bank[5:7]
        acc = bank[7]
        T_BANK = [gp[0], gp[1], sc[0], sc[1], gp[2], pt[0], gp[0], gp[1]]
        V_BANK = [pt[1], pt[0], gp[0], gp[1]] * 2
        AT_BANK = [gp[2], gp[2]]
        L1_BANK = [gp[n % 3] for n in range(2 * KC)]
        L2_BANK = [gp[2], gp[0], gp[1], gp[2]]
        L3_BANK = [gp[0], gp[1], gp[2], gp[0]]
        L4_BANK, YT_BANK, XT_BANK, X1T_BANK = gp[1], gp[2], gp[1], gp[2]

        (s_wqk, s_wv, s_wf, s_ident, s_prep_mm, s_prep_hi, s_prep_lo, s_lomax, s_flagt, s_flag,
         s_zero, s_scales_mm, s_scales, s_held) = (sem(n) for n in (
            "wqk_in", "wv_in", "wf_in", "ident_made", "prep_mm", "prep_hi", "prep_lo", "lomax_made",
            "flag_turned", "flag_made", "zeroed", "scales_mm", "scales_ready", "held"))
        s_xin, s_res, s_yfree = sem("x_in_landed"), sem("res_landed"), sem("y_free")
        s_xt_mm, s_xt_hi, s_xt_lo = sem("xt_mm"), sem("xt_hi"), sem("xt_lo")
        s_t_mm, s_t_hi, s_t_lo = sem("t_mm"), sem("t_hi"), sem("t_lo")
        s_v_mm, s_v_hi, s_v_lo = sem("v_mm"), sem("v_hi"), sem("v_lo")
        s_sc, s_max, s_exp, s_inv, s_norm = (sem(n) for n in ("scores", "max", "exp", "inv", "norm"))
        s_pt_mm, s_pt_hi, s_pt_lo, s_pv = (sem(n) for n in ("pt_mm", "pt_hi", "pt_lo", "pv"))
        s_acc, s_at, s_radd = sem("acc_copied"), sem("at_mm"), sem("res_added")
        s_ve1, s_rs1, s_x1 = sem("var_eps1"), sem("rstd1"), sem("x1_ready")
        s_st1, s_mv1, s_st2, s_mv2 = sem("stats1"), sem("mv1"), sem("stats2"), sem("mv2")
        s_x1t_mm, s_x1t_hi, s_x1t_lo = sem("x1t_mm"), sem("x1t_hi"), sem("x1t_lo")
        s_z1, s_z2, s_silu, s_gate = sem("z1"), sem("z2"), sem("silu"), sem("gate")
        s_l2, s_l3 = sem("l2_mm"), sem("l3_mm")
        s_1hi, s_1lo, s_2hi, s_2lo, s_3hi, s_3lo = (
            sem(f"l{n}_{s}") for n in (1, 2, 3) for s in ("hi", "lo"))
        s_l4, s_yt, s_yt_mm, s_yadd = sem("l4_mm"), sem("yt_ready"), sem("yt_mm"), sem("y_added")
        s_ve2, s_rs2, s_y = sem("var_eps2"), sem("rstd2"), sem("y_ready")

        block = ctx.enter_context(nc.Block())

        def steps(eng, step):
            step(0, None, False)
            with eng.Fori(1, PAIRS - 1) as i:
                step(i, i - 1, False)
            step(PAIRS - 1, PAIRS - 2, True)
            step(None, PAIRS - 1, True)

        G_FFN = 4
        PREP = [(a_hi[:, 0:4, :], a_lo[:, 0:4, :]), (a_hi[:, 4:8, :], a_lo[:, 4:8, :]),
                (wv_hi[:, 0:512], wv_lo[:, 0:512]), (wv_hi[:, 512:1024], wv_lo[:, 512:1024]),
                (w1_hi[:, :], w1_lo[:, :]), (w2_hi[:, :], w2_lo[:, :])]
        PREP += [(h1_hi[:, c, :], h1_lo[:, c, :]) for c in range(KC)]
        PREP += [(h2_hi[:, c, :], h2_lo[:, c, :]) for c in range(KC)]
        PREP += [(w3_hi[:, :, :], w3_lo[:, :, :])]
        NPREP = len(PREP)

        def hold(eng, s, value):
            eng.wait_ge(s, value)
            eng.sem_inc(s_held)

        def prep_bank(g, like):
            b = bank[g % 8][:, :]
            return b.rearrange("p (c n) -> p c n", n=D) if len(like.shape) == 3 else b

        @block.sync
        def _(sp):
            sp.dma_start(x_in[:, :, :], x_rows[0]).then_inc(s_xin, 16)
            sp.dma_start(wq_in[:, :, :], wq.rearrange("(h r) d -> r h d", h=H)).then_inc(s_wqk, 16)
            sp.dma_start(wk_in[:, :, :], wk.rearrange("(h r) d -> r h d", h=H)).then_inc(s_wqk, 16)
            sp.dma_start(wv_in[:, :, :], wv.rearrange("(h p) d -> p h d", h=H)).then_inc(s_wv, 16)
            sp.dma_start(w1_in[:, :, :], w1_w.rearrange("(c p) d -> p c d", p=P)).then_inc(s_wf, 16)
            sp.dma_start(w2_in[:, :, :], w2_w.rearrange("(c p) d -> p c d", p=P)).then_inc(s_wf, 16)
            sp.dma_start(h1_in[:, :, :], h1_w.rearrange("(c p) d -> p c d", p=P)).then_inc(s_wf, 16)
            sp.dma_start(h2_in[:, :, :], h2_w.rearrange("(c p) d -> p c d", p=P)).then_inc(s_wf, 16)
            sp.dma_start(w3_in[:, :], w3_w).then_inc(s_wf, 16)
            for n, s in enumerate((w1_s, w2_s, h1_s, h2_s)):
                sp.dma_start(scales_in[n * KC:(n + 1) * KC, :], s.rearrange("(c p) -> c p", p=P)).then_inc(s_wf, 16)
            for n in (4 * KC, 4 * KC + 1):
                sp.dma_start(scales_in[n:n + 1, :], w3_s.rearrange("(a p) -> a p", a=1)).then_inc(s_wf, 16)
            sp.dma_start(res[:, :, :], x_rows[0]).then_inc(s_res, 16)

            def step(i, f, last):
                if i is not None and not last:
                    sp.wait_ge(s_xt_mm, i + 1)
                    sp.dma_start(x_in[:, :, :], x_rows[i + 1]).then_inc(s_xin, 16)
                if f is not None:
                    if i is not None:
                        sp.wait_ge(s_x1, 2 * f + 2)
                        sp.dma_start(res[:, :, :], x_rows[i]).then_inc(s_res, 16)
                    sp.wait_ge(s_y, f + 1)
                    sp.dma_start(out_rows[f], y[:, :, :]).then_inc(s_yfree, 16)

            steps(sp, step)
            sp.wait_ge(s_yfree, 16 * (PAIRS + 1))

        @block.gpsimd
        def _(pool):
            nc.gpsimd.memset(ident[:, :], 0.0).then_inc(s_zero, 1)
            nc.gpsimd.memset(minus_half[:, :], -0.5).then_inc(s_zero, 1)
            nc.gpsimd.memset(y[:, :, :], 0.0).then_inc(s_yfree, 16)
            pool.wait_ge(s_zero, 1)
            nc.gpsimd.affine_select(out=ident[:, :], in_=ident[:, :], compare_op=ALU.not_equal, fill=1.0,
                                    base=0, pattern=[[-1, P]], channel_multiplier=1).then_inc(s_ident, 1)

            def norm(i, j):
                pool.wait_ge(s_inv, i * J + j + 1)
                nc.gpsimd.tensor_tensor(prob[:, j % PRING, :, :], prob[:, j % PRING, :, :],
                                        inv_total[:, j % PRING, :].unsqueeze(2).to_broadcast([P, NT, N]),
                                        ALU.mult).then_inc(s_norm, 1)

            def lo_part(f, c, hi, lo, s_in, s_lo):
                pool.wait_ge(s_in, f * KC + c + 1)
                nc.gpsimd.tensor_tensor(lo[:, c, :], act32[:, c % RING, :], hi[:, c, :].bitcast(F32),
                                        ALU.subtract).then_inc(s_lo, 1)

            def layer_norm(count, first, n, src, dst, mv, var_eps, rstd, s_mv, s_ve, s_rs, s_out):
                tiles = slice(first, first + n)
                hold(pool, s_mv, (count + 1) * n)
                nc.gpsimd.tensor_scalar(var_eps[:, tiles], mv[:, tiles, 1], EPS, None,
                                        ALU.add).then_inc(s_ve, 1)
                pool.wait_ge(s_ve, count + 1)
                nc.gpsimd.tensor_tensor(rstd[:, tiles], var_eps[:, tiles], minus_half[:, tiles],
                                        ALU.pow).then_inc(s_rs, 1)
                hold(pool, s_rs, count + 1)
                for t in range(first, first + n):
                    last = nc.gpsimd.tensor_scalar(dst[:, t, :], src[:, t, :], mv[:, t, 0:1],
                                                   rstd[:, t:t + 1], ALU.subtract, ALU.mult)
                last.then_inc(s_out, 1)

            def norm1(f, b):
                layer_norm(2 * f + b, NT * b, NT, res, x1, mv1, var_eps1, rstd1, s_mv1, s_ve1, s_rs1, s_x1)

            def step(i, f, last):
                if f is not None:
                    norm1(f, 1)
                if i is not None:
                    for j in range(LEAD - 1):
                        norm(i, j)
                for j in range(J):
                    if i is not None and j + LEAD - 1 < J:
                        norm(i, j + LEAD - 1)
                    if f is None:
                        continue
                    for c in {L1_SLOT + 1: (0, 1), L1_SLOT + 2: (2, 3)}.get(j, ()):
                        lo_part(f, c, odd_hi, odd_lo, s_1hi, s_1lo)
                    for c in {L2_SLOT: (0,), L2_SLOT + 1: (1, 2), L2_SLOT + 2: (3,)}.get(j, ()):
                        lo_part(f, c, even_hi, even_lo, s_2hi, s_2lo)
                    for c in {L3_SLOT: (0,), L3_SLOT + 1: (1, 2), L3_SLOT + 2: (3,)}.get(j, ()):
                        lo_part(f, c, odd_hi, odd_lo, s_3hi, s_3lo)
                if f is not None:
                    pool.wait_ge(s_yfree, 16 * (f + 1))
                    layer_norm(f, 0, TT, x1, y, mv2, var_eps2, rstd2, s_mv2, s_ve2, s_rs2, s_y)
                if i is not None:
                    norm1(i, 0)

            steps(pool, step)

        @block.scalar
        def _(act):
            def copy(dst, src):
                return nc.scalar.activation(dst, src, ACT.Copy)

            for g, (hi, _lo) in enumerate(PREP):
                act.wait_ge(s_prep_mm, g + 1)
                copy(hi, prep_bank(g, hi)).then_inc(s_prep_hi, 1)
            act.wait_ge(s_scales_mm, 1)
            copy(scales[:, :], acc[:, 0:NSC]).then_inc(s_scales, 1)
            act.wait_ge(s_scales, 1)

            def xt_part(i):
                act.wait_ge(s_xt_mm, i + 1)
                copy(xt_hi[:, :], XT_BANK[:, :]).then_inc(s_xt_hi, 1)

            def acc_copy(i, b):
                act.wait_ge(s_pv, i * J + (b + 1) * H)
                if b == 1:
                    act.wait_ge(s_at, 2 * i + 1)
                elif not isinstance(i, int) or i > 0:
                    act.wait_ge(s_at, 2 * i)
                copy(at[:, :], acc[:, b * N:(b + 1) * N]).then_inc(s_acc, 1)

            def exp(i, j):
                act.wait_ge(s_max, i * J + j + 1)
                if j >= PRING:
                    act.wait_ge(s_pt_mm, i * J + j - PRING + 1)
                for nt in range(NT):
                    last = nc.scalar.activation(prob[:, j % PRING, nt, :], sc[j % 2][:, nt * N:(nt + 1) * N],
                                                ACT.Exp, bias=neg_max[:, j % PRING, nt:nt + 1],
                                                accum_out=total[:, j % PRING, nt:nt + 1])
                last.then_inc(s_exp, 1)

            def pt_part(i, j):
                act.wait_ge(s_pt_mm, i * J + j + 1)
                if j >= RING:
                    act.wait_ge(s_pv, i * J + j - RING + 1)
                copy(pt_hi[:, j % RING, :, :], pt[j % 2].rearrange("p (t n) -> p t n", n=N)).then_inc(s_pt_hi, 1)

            def v_part(i, v):
                act.wait_ge(s_v_mm, i * VT + v + 1)
                copy(v_hi[:, v // 2, (v % 2) * 512:(v % 2 + 1) * 512], V_BANK[v][:, :]).then_inc(s_v_hi, 1)

            def gelus(f, chunks, banks, n_scale, hi, s_mm, s_out, s_lo):
                for c in chunks:
                    act.wait_ge(s_mm, f * KC + c + 1)
                    if c >= RING:
                        act.wait_ge(s_lo, f * KC + c - RING + 1)
                    for dst in (act32[:, c % RING, :], hi[:, c, :]):
                        last = nc.scalar.activation(dst, banks[c][:, :], ACT.Gelu,
                                                    scale=scales[:, n_scale * KC + c:n_scale * KC + c + 1])
                    last.then_inc(s_out, 1)

            def silus(f, chunks):
                for c in chunks:
                    act.wait_ge(s_z1, f * KC + c + 1)
                    if c >= 2:
                        act.wait_ge(s_gate, f * KC + c - 1)
                    nc.scalar.activation(silu_out[:, c % 2, :], L1_BANK[2 * c][:, :], ACT.Silu,
                                         scale=scales[:, c:c + 1]).then_inc(s_silu, 1)

            xt_part(0)

            def step(i, f, last):
                if f is not None:
                    acc_copy(f, 1)
                if i is not None:
                    for h in range(H):
                        act.wait_ge(s_t_mm, i * H + h + 1)
                        copy(t_hi[:, h, :], T_BANK[h][:, :]).then_inc(s_t_hi, 1)
                    for v in range(VT):
                        if v % 2 == 0 and v < 2 * LEAD:
                            exp(i, v // 2)
                        v_part(i, v)
                for j in range(J):
                    second = j in (L1_SLOT + 1, L2_SLOT + 1, L3_SLOT + 1) and f is not None
                    if i is not None:
                        pt_part(i, j)
                        if j + LEAD < J and not second:
                            exp(i, j + LEAD)
                    if j == 0 and f is not None:
                        act.wait_ge(s_x1t_mm, f + 1)
                        copy(x1t_hi[:, :], X1T_BANK[:, :]).then_inc(s_x1t_hi, 1)
                    if i is not None and j == H + 1:
                        acc_copy(i, 0)
                    if f is not None:
                        if j in (L1_SLOT, L1_SLOT + 1):
                            silus(f, (0, 1) if j == L1_SLOT else (2, 3))
                        if j in (L2_SLOT, L2_SLOT + 1):
                            gelus(f, (0, 1) if j == L2_SLOT else (2, 3), L2_BANK, 2, even_hi, s_l2, s_2hi, s_2lo)
                        if j in (L3_SLOT, L3_SLOT + 1):
                            gelus(f, (0, 1) if j == L3_SLOT else (2, 3), L3_BANK, 3, odd_hi, s_l3, s_3hi, s_3lo)
                        if j == L4_SLOT:
                            act.wait_ge(s_l4, f + 1)
                            nc.scalar.activation(yt[:, :], L4_BANK[:, :], ACT.Copy,
                                                 scale=scales[:, 4 * KC:4 * KC + 1]).then_inc(s_yt, 1)
                    if i is not None and j + LEAD < J and second:
                        exp(i, j + LEAD)
                if i is not None and not last:
                    xt_part(i + 1)

            steps(act, step)

        @block.vector
        def _(dve):
            def minus(dst, src, hi):
                return nc.vector.tensor_tensor(dst, src, hi.bitcast(F32), ALU.subtract)

            for g, (hi, lo) in enumerate(PREP):
                dve.wait_ge(s_prep_hi, g + 1)
                minus(lo, prep_bank(g, lo), hi).then_inc(s_prep_lo, 1)

            def xt_part(i):
                dve.wait_ge(s_xt_hi, i + 1)
                minus(xt_lo[:, :], XT_BANK[:, :], xt_hi[:, :]).then_inc(s_xt_lo, 1)

            def flag():
                dve.wait_ge(s_prep_lo, NPREP)
                for n, lo in enumerate((w1_lo[:, :], w2_lo[:, :], h1_lo[:, :, :], h2_lo[:, :, :], w3_lo[:, :, :])):
                    nc.vector.tensor_reduce(lo_max[:, n:n + 1], lo.bitcast(F32), AX.X if n < 2 else AX.XY,
                                            ALU.max, apply_absolute_value=True).then_inc(s_lomax, 1)
                dve.wait_ge(s_lomax, 5)
                nc.vector.tensor_reduce(lo_max[:, 5:6], lo_max[:, 0:5], AX.X, ALU.max).then_inc(s_lomax, 1)
                dve.wait_ge(s_flagt, 1)
                nc.vector.tensor_reduce(lo_flag[0:1, 0:1], acc[0:1, 0:P], AX.X, ALU.max).then_inc(s_flag, 1)

            def res_add(i, b):
                dve.wait_ge(s_at, 2 * i + b + 1)
                if b == 0:
                    dve.wait_ge(s_res, 16 * (i + 1))
                half = res[:, NT * b:NT * (b + 1), :]
                nc.vector.tensor_tensor(half, AT_BANK[b][:, 0:N].rearrange("p (t d) -> p t d", d=D), half,
                                        ALU.add).then_inc(s_radd, 1)
                dve.wait_ge(s_radd, 2 * i + b + 1)
                for t in range(NT * b, NT * (b + 1)):
                    nc.vector.bn_stats(stats1[:, t, :], res[:, t, :]).then_inc(s_st1, 1)
                for t in range(NT * b, NT * (b + 1)):
                    hold(dve, s_st1, i * TT + t + 1)
                    nc.vector.bn_aggr(mv1[:, t, :], stats1[:, t, :]).then_inc(s_mv1, 1)

            def row_max(i, j):
                dve.wait_ge(s_sc, i * J + j + 1)
                nc.vector.tensor_reduce(neg_max[:, j % PRING, :], sc[j % 2].rearrange("p (t m) -> p t m", m=N),
                                        AX.X, ALU.max, negate=True).then_inc(s_max, 1)

            def inverse(i, j):
                dve.wait_ge(s_exp, i * J + j + 1)
                nc.vector.reciprocal(inv_total[:, j % PRING, :], total[:, j % PRING, :]).then_inc(s_inv, 1)

            def l1_hi(f, c):
                dve.wait_ge(s_gate, f * KC + c + 1)
                nc.vector.tensor_copy(odd_hi[:, c, :], act32[:, c % RING, :]).then_inc(s_1hi, 1)

            xt_part(0)
            flag()

            def gates(f, chunks):
                for c in chunks:
                    dve.wait_ge(s_silu, f * KC + c + 1)
                    dve.wait_ge(s_z2, f * KC + c + 1)
                    if c >= RING:
                        dve.wait_ge(s_1lo, f * KC + c - RING + 1)
                    nc.vector.scalar_tensor_tensor(
                        out=act32[:, c % RING, :], in0=L1_BANK[2 * c + 1][:, :], scalar=scales[:, KC + c:KC + c + 1],
                        in1=silu_out[:, c % 2, :], op0=ALU.mult, op1=ALU.mult).then_inc(s_gate, 1)
                    if c >= 1:
                        l1_hi(f, c - 1)
                if KC - 1 in chunks:
                    l1_hi(f, KC - 1)

            def step(i, f, last):
                if i is not None:
                    for h in range(H):
                        dve.wait_ge(s_t_hi, i * H + h + 1)
                        minus(t_lo[:, h, :], T_BANK[h][:, :], t_hi[:, h, :]).then_inc(s_t_lo, 1)
                    row_max(i, 0)
                    row_max(i, 1)
                if f is not None:
                    res_add(f, 1)
                if i is not None:
                    for v in range(VT):
                        if v == 3:
                            row_max(i, 2)
                        if v in (2, 4):
                            inverse(i, v // 2 - 1)
                        dve.wait_ge(s_v_hi, i * VT + v + 1)
                        cols = slice((v % 2) * 512, (v % 2 + 1) * 512)
                        minus(v_lo[:, v // 2, cols], V_BANK[v][:, :], v_hi[:, v // 2, cols]).then_inc(s_v_lo, 1)
                for j in range(J):
                    if i is not None:
                        if j + LEAD < J:
                            row_max(i, j + LEAD)
                        if j + LEAD - 1 < J:
                            inverse(i, j + LEAD - 1)
                        dve.wait_ge(s_pt_hi, i * J + j + 1)
                        minus(pt_lo[:, j % RING, :, :], pt[j % 2].rearrange("p (t n) -> p t n", n=N),
                              pt_hi[:, j % RING, :, :]).then_inc(s_pt_lo, 1)
                    if j == 0 and f is not None:
                        dve.wait_ge(s_x1t_hi, f + 1)
                        minus(x1t_lo[:, :], X1T_BANK[:, :], x1t_hi[:, :]).then_inc(s_x1t_lo, 1)
                    if j == AT0_SLOT and i is not None:
                        res_add(i, 0)
                    if j in (L1_SLOT, L1_SLOT + 1) and f is not None:
                        gates(f, (0,) if j == L1_SLOT else (1, 2, 3))
                if i is not None and not last:
                    xt_part(i + 1)
                if f is not None:
                    dve.wait_ge(s_yt_mm, f + 1)
                    nc.vector.tensor_tensor(x1[:, :, :], YT_BANK.rearrange("p (t d) -> p t d", d=D), x1[:, :, :],
                                            ALU.add).then_inc(s_yadd, 1)
                    dve.wait_ge(s_yadd, f + 1)
                    for t in range(TT):
                        nc.vector.bn_stats(stats2[:, t, :], x1[:, t, :]).then_inc(s_st2, 1)
                    for t in range(TT):
                        hold(dve, s_st2, f * TT + t + 1)
                        nc.vector.bn_aggr(mv2[:, t, :], stats2[:, t, :]).then_inc(s_mv2, 1)

            steps(dve, step)

        @block.tensor
        def _(pe):
            mm, turn = nc.tensor.matmul, nc.tensor.transpose

            def three(dst, w_hi, w_lo, m_hi, m_lo, start, stop):
                mm(dst, w_hi, m_hi, start=start, stop=False)
                mm(dst, w_hi, m_lo, start=False, stop=False)
                return mm(dst, w_lo, m_hi, start=False, stop=stop)

            def turns(dst, blocks, s_out):
                for n, b in enumerate(blocks):
                    last = turn(dst[:, n * P:(n + 1) * P], b, ident[:, :])
                last.then_inc(s_out, 1)

            def turn_x(i):
                pe.wait_ge(s_xin, 16 * (i + 1))
                turns(XT_BANK, [x_in[:, t, :] for t in range(TT)], s_xt_mm)

            pe.wait_ge(s_wqk, 32)
            for g in range(2):
                for h in range(4):
                    last = mm(bank[g][:, h * D:(h + 1) * D], wq_in[:, 4 * g + h, :], wk_in[:, 4 * g + h, :],
                              start=True, stop=True)
                last.then_inc(s_prep_mm, 1)
            pe.wait_ge(s_ident, 1)
            pe.wait_ge(s_wv, 16)
            for g in range(2):
                turns(bank[2 + g], [wv_in[:, 4 * g + h, :] for h in range(4)], s_prep_mm)
            pe.wait_ge(s_wf, 16 * 11)
            blocks = [[w1_in[:, c, :] for c in range(KC)], [w2_in[:, c, :] for c in range(KC)]]
            for w in (h1_in, h2_in):
                blocks += [[w[:, o, c * P:(c + 1) * P] for o in range(KC)] for c in range(KC)]
            blocks += [[w3_in[:, c * P:(c + 1) * P] for c in range(KC)]]
            for n, b in enumerate(blocks):
                g = G_FFN + n
                if g >= 8:
                    pe.wait_ge(s_prep_lo, g - 7)
                turns(bank[g % 8], b, s_prep_mm)
            pe.wait_ge(s_prep_lo, NPREP)
            turn_x(0)
            turn(acc[:, 0:NSC], scales_in[:, :], ident[0:NSC, 0:NSC]).then_inc(s_scales_mm, 1)
            pe.wait_ge(s_scales, 1)
            pe.wait_ge(s_lomax, 6)
            turn(acc[0:1, 0:P], lo_max[:, 5:6], ident[:, :]).then_inc(s_flagt, 1)
            pe.wait_ge(s_flag, 1)
            any_lo = pe.value_load(lo_flag[0:1, 0:1].bitcast(I32))

            def layer(o, dst, w_hi, w_lo, m_hi, m_lo, s_parts, f, with_lo):
                n = len(w_hi)
                for c in range(n):
                    if s_parts is not None and o == 0:
                        pe.wait_ge(s_parts, f * KC + c + 1)
                    mm(dst, w_hi[c], m_hi[c], start=(c == 0), stop=False)
                    last = mm(dst, w_hi[c], m_lo[c], start=False, stop=(c == n - 1 and not with_lo))
                    if with_lo:
                        last = mm(dst, w_lo[c], m_hi[c], start=False, stop=(c == n - 1))
                return last

            def either(emit):
                with pe.If(any_lo):
                    emit(True)
                with pe.Else():
                    emit(False)

            def layer1(i, f, products, with_lo):
                for n in products:
                        o = n // 2
                        cols = slice(o * P, (o + 1) * P)
                        hi, lo, s_out = (w2_hi, w2_lo, s_z2) if n % 2 else (w1_hi, w1_lo, s_z1)
                        if n == 0:
                            pe.wait_ge(s_x1t_lo, f + 1)
                        if n in (0, 1) and i is not None:
                            pe.wait_ge(s_v_lo, i * VT + VT - 1 + n)
                        if n >= 3:
                            m = (n - 3) // 2
                            pe.wait_ge(s_gate if (n - 3) % 2 else s_silu, f * KC + m + 1)
                        layer(o, L1_BANK[n][:, :], [hi[:, cols]], [lo[:, cols]], [x1t_hi[:, :]],
                              [x1t_lo[:, :]], None, f, with_lo).then_inc(s_out, 1)

            def layer23(f, chunks, banks, w_hi, w_lo, m_hi, m_lo, s_prior, n_prior, s_parts, s_free, s_out, with_lo):
                for o in chunks:
                    cols = slice(o * P, (o + 1) * P)
                    if o == 0:
                        pe.wait_ge(s_prior, f * KC + n_prior)
                    if o == KC - 1:
                        pe.wait_ge(s_free, f * KC + 1)
                    layer(o, banks[o][:, :], [w_hi[:, c, cols] for c in range(KC)],
                          [w_lo[:, c, cols] for c in range(KC)], [m_hi[:, c, :] for c in range(KC)],
                          [m_lo[:, c, :] for c in range(KC)], s_parts, f, with_lo).then_inc(s_out, 1)

            def layer4(f, with_lo):
                pe.wait_ge(s_3hi, f * KC + 2)
                layer(0, L4_BANK[:, :], [w3_hi[:, c, :] for c in range(KC)], [w3_lo[:, c, :] for c in range(KC)],
                      [odd_hi[:, c, :] for c in range(KC)], [odd_lo[:, c, :] for c in range(KC)],
                      s_3lo, f, with_lo).then_inc(s_l4, 1)

            def project_t(i):
                pe.wait_ge(s_xt_lo, i + 1)
                for h in range(H):
                    if h == 4:
                        pe.wait_ge(s_t_lo, i * H + 1)
                    if h >= 6:
                        pe.wait_ge(s_t_lo, i * H + h - 5)
                    three(T_BANK[h][:, :], a_hi[:, h, :], a_lo[:, h, :], xt_hi[:, :], xt_lo[:, :],
                          True, True).then_inc(s_t_mm, 1)

            def project_v(i, tiles):
                for v in tiles:
                    if 1 <= v < 4:
                        pe.wait_ge(s_t_lo, i * H + 5 + v)
                    if v >= 4:
                        pe.wait_ge(s_v_lo, i * VT + v - 3)
                    rows = slice((v // 2) * P, (v // 2 + 1) * P)
                    cols = slice((v % 2) * 512, (v % 2 + 1) * 512)
                    three(V_BANK[v][:, :], xt_hi[:, rows], xt_lo[:, rows], wv_hi[:, cols], wv_lo[:, cols],
                          True, True).then_inc(s_v_mm, 1)

            def scores(i, j):
                b, h = j // H, j % H
                if j < H:
                    pe.wait_ge(s_t_lo, i * H + max(h + 1, j + 3 if j < 2 else 0))
                if j >= 2:
                    pe.wait_ge(s_exp, i * J + j - 1)
                for nt in range(NT):
                    q = slice(b * N + nt * P, b * N + (nt + 1) * P)
                    m = slice(b * N, (b + 1) * N)
                    last = three(sc[j % 2][:, nt * N:(nt + 1) * N], t_hi[:, h, q], t_lo[:, h, q],
                                 xt_hi[:, m], xt_lo[:, m], True, True)
                last.then_inc(s_sc, 1)

            def turn_prob(i, j):
                pe.wait_ge(s_norm, i * J + j + 1)
                if j < 2:
                    pe.wait_ge(s_v_lo, i * VT + 6 - j)
                else:
                    pe.wait_ge(s_pt_lo, i * J + j - 1)
                turns(pt[j % 2], [prob[:, j % PRING, nt, mt * P:(mt + 1) * P]
                                  for mt in range(NT) for nt in range(NT)], s_pt_mm)

            def times_v(i, j):
                b, h = j // H, j % H
                pe.wait_ge(s_pt_lo, i * J + j + 1)
                if j == 0:
                    pe.wait_ge(s_v_lo, (i + 1) * VT)
                if j == H:
                    pe.wait_ge(s_acc, 2 * i + 1)
                for mt in range(NT):
                    v = slice(h * D, (h + 1) * D)
                    last = three(acc[:, b * N:(b + 1) * N], v_hi[:, b * NT + mt, v], v_lo[:, b * NT + mt, v],
                                 pt_hi[:, j % RING, mt, :], pt_lo[:, j % RING, mt, :],
                                 h == 0 and mt == 0, h == H - 1 and mt == NT - 1)
                last.then_inc(s_pv, 1)

            def turn_attention(i, b):
                pe.wait_ge(s_acc, 2 * i + b + 1)
                turns(AT_BANK[b], [at[:, t * P:(t + 1) * P] for t in range(NT)], s_at)

            def ffn_part(i, f, j):
                if j in (L1_SLOT, L1_SLOT + 1):
                    n = range(0, 3) if j == L1_SLOT else range(3, 2 * KC)
                    either(lambda w: layer1(i, f, n, w))
                if j in (L2_SLOT, L2_SLOT + 1):
                    o = (0, 1) if j == L2_SLOT else (2, 3)
                    either(lambda w: layer23(f, o, L2_BANK, h1_hi, h1_lo, odd_hi, odd_lo, s_gate, 3, s_1lo, s_2hi, s_l2, w))
                if j in (L3_SLOT, L3_SLOT + 1):
                    o = (0, 1) if j == L3_SLOT else (2, 3)
                    either(lambda w: layer23(f, o, L3_BANK, h2_hi, h2_lo, even_hi, even_lo, s_2hi, 2, s_2lo, s_3hi, s_l3, w))
                if j == L4_SLOT:
                    either(lambda w: layer4(f, w))

            def step(i, f, last):
                if i is not None:
                    project_t(i)
                if f is not None:
                    if i is not None:
                        pe.wait_ge(s_t_lo, i * H + 5)
                    else:
                        pe.wait_ge(s_yadd, f)
                    turn_attention(f, 1)
                if i is not None:
                    scores(i, 0)
                    scores(i, 1)
                    project_v(i, range(0, 4))
                    scores(i, 2)
                    project_v(i, range(4, VT))
                for j in range(J):
                    if i is not None:
                        if j + LEAD < J:
                            scores(i, j + LEAD)
                        turn_prob(i, j)
                        if j == J - 1 and not last:
                            if f is not None:
                                pe.wait_ge(s_yt, f + 1)
                            turn_x(i + 1)
                        if j >= 2:
                            times_v(i, j - 2)
                    if f is not None:
                        if j == 0:
                            pe.wait_ge(s_x1, 2 * f + 2)
                            turns(X1T_BANK, [x1[:, t, :] for t in range(TT)], s_x1t_mm)
                        ffn_part(i, f, j)
                    if j == AT0_SLOT and i is not None:
                        if f is not None:
                            pe.wait_ge(s_3hi, f * KC + 3)
                        turn_attention(i, 0)
                if f is not None:
                    if i is not None:
                        pe.wait_ge(s_radd, 2 * i + 1)
                    pe.wait_ge(s_yt, f + 1)
                    turns(YT_BANK, [yt[:, t * P:(t + 1) * P] for t in range(TT)], s_yt_mm)
                if i is not None:
                    times_v(i, J - 2)
                    times_v(i, J - 1)

            steps(pe, step)


_INS = ["L0_attn_x", "L0_attn_Wq", "L0_attn_Wk", "L0_attn_Wv", "L0_ffn_w1_w", "L0_ffn_w1_s", "L0_ffn_w2_w",
        "L0_ffn_w2_s", "L0_ffn_h1_w", "L0_ffn_h1_s", "L0_ffn_h2_w", "L0_ffn_h2_s", "L0_ffn_w3_w", "L0_ffn_w3_s"]


def kernel(**inputs):
    import numpy as np
    import concourse.bacc as bacc
    from concourse.bass_utils import run_bass_kernel_spmd

    nc = bacc.Bacc("TRN2", target_bir_lowering=False, num_devices=1)
    arrays, args = {}, []
    for name in _INS:
        a = np.ascontiguousarray(inputs[name])
        arrays[f"in_{name}"] = a
        args.append(nc.dram_tensor(f"in_{name}", a.shape, mybir.dt.from_np(a.dtype), kind="ExternalInput").ap())
    shape = arrays["in_L0_attn_x"].shape
    args.append(nc.dram_tensor("out_x", shape, F32, kind="ExternalOutput").ap())
    layer_kernel(nc, *args)
    r = run_bass_kernel_spmd(nc, [arrays], core_ids=[0])
    return r.results[0]["out_x"]
```

```python
from contextlib import ExitStack

import concourse.bass as bass
from concourse import mybir

F32 = mybir.dt.float32
F32R = mybir.dt.float32r
I32 = mybir.dt.int32
ACT = mybir.ActivationFunctionType
ALU = mybir.AluOpType
AX = mybir.AxisListType

P = 128
D = 128
HID = 512
KC = HID // P
EPS = 1e-5
LEAD = 3
LAG = 2
RING = 4
AT1_SLOT = 2
NORM1_SLOTS = (0, 3)
X1T_SLOT = 4
L1_SLOTS = (5, 6, 7, 8)
L2_SLOT = 9
AT0_SLOT = 10
STATS1_SLOT = 14
L3_SLOT = 12
XT_SLOT = 14
L4_SLOT = 14
YT_SLOT = 15
NORM2_SLOT = 9


TILES_BEFORE = ((0, 1, 2), (3,), (4, 5), (6, 7))


def count(i, per, more):
    reg, off = i
    fixed = off * per + more
    return fixed if reg is None else reg * per + fixed


def plus(i, n):
    return i[0], i[1] + n


def is_first(i):
    return i[0] is None and i[1] == 0


def need(eng, sem, value):
    if not isinstance(value, int) or value > 0:
        eng.wait_ge(sem, value)


def layer_kernel(nc, x, wq, wk, wv, w1_w, w1_s, w2_w, w2_s, h1_w, h1_s, h2_w, h2_s, w3_w, w3_s, out):
    B, N, _ = x.shape
    H = wv.shape[0] // D
    R = wq.shape[0] // H
    PAIRS = B // 2
    TOK = 2 * N
    TT = TOK // P
    NT = N // P
    J = 2 * H
    VT = TT * H * D // TOK
    V_ORDER = [(0, 0), (1, 0), (0, 1), (1, 1), (2, 0), (3, 0), (2, 1), (3, 1)]
    V_OF_UNIT = {0: 2, H // 2: 4, H: 6, H + H // 2: 8}

    x_rows = x.rearrange("(i b) (t p) d -> i p (b t) d", b=2, p=P)
    out_rows = out.rearrange("(i b) (t p) d -> i p (b t) d", b=2, p=P)

    def exists(i):
        return i[0] is not None or i[1] < PAIRS

    def row(i):
        return i[1] if i[0] is None else i[0] + i[1]

    with ExitStack() as ctx:
        def sb(name, shape, dt=F32, at=None):
            return (at or ctx).enter_context(nc.sbuf_tensor(name, shape, dt))

        def sem(name):
            return ctx.enter_context(nc.semaphore(name))

        ident = sb("ident", [P, P])
        minus_half = sb("minus_half", [P, TT])
        NSC = 4 * KC + 2
        scales = sb("scales", [P, NSC])
        half_s1 = sb("half_s1", [P, KC])
        half_s12 = sb("half_s12", [P, KC])
        a_hi, a_lo = (sb(f"a_{s}", [P, H, D], F32R) for s in ("hi", "lo"))
        wv_hi, wv_lo = (sb(f"wv_{s}", [P, H * D], F32R) for s in ("hi", "lo"))
        w1_hi, w1_lo = (sb(f"w1_{s}", [P, HID], F32R) for s in ("hi", "lo"))
        w2_hi, w2_lo = (sb(f"w2_{s}", [P, HID], F32R) for s in ("hi", "lo"))
        h1_hi, h1_lo = (sb(f"h1_{s}", [P, KC, HID], F32R) for s in ("hi", "lo"))
        h2_hi, h2_lo = (sb(f"h2_{s}", [P, KC, HID], F32R) for s in ("hi", "lo"))
        w3_hi, w3_lo = (sb(f"w3_{s}", [P, KC, D], F32R) for s in ("hi", "lo"))

        with ExitStack() as early:
            wq_in = sb("wq_in", [R, H, D], at=early)
            wk_in = sb("wk_in", [R, H, D], at=early)
            wv_in = sb("wv_in", [P, H, D], at=early)
        v_hi, v_lo = (sb(f"v_{s}", [P, TT, H * D], F32R) for s in ("hi", "lo"))
        t_hi, t_lo = (sb(f"t_{s}", [P, H, TOK], F32R) for s in ("hi", "lo"))
        prob = sb("prob", [P, RING, NT, N])
        pt_hi, pt_lo = (sb(f"pt_{s}", [P, RING, NT, N], F32R) for s in ("hi", "lo"))
        neg_max = sb("neg_max", [P, RING, NT])
        total = sb("total", [P, RING, NT])
        inv_total = sb("inv_total", [P, RING, NT])
        x_in = sb("x_in", [P, TT, D])
        res = sb("res", [P, TT, D])
        xt_hi, xt_lo = ([sb(f"xt_{s}{n}", [P, TOK], F32R) for n in range(2)] for s in ("hi", "lo"))
        x1 = sb("x1", [P, TT, D])
        y = sb("y", [P, TT, D])
        stats1, stats2 = (sb(f"stats{n}", [P, TT, 6]) for n in (1, 2))
        var_eps1, var_eps2 = (sb(f"var_eps{n}", [P, TT]) for n in (1, 2))
        mv1, mv2 = (sb(f"mv{n}", [P, TT, 2]) for n in (1, 2))
        rstd1, rstd2 = (sb(f"rstd{n}", [P, TT]) for n in (1, 2))

        with ExitStack() as early:
            w1_in = sb("w1_in", [P, KC, D], at=early)
            w2_in = sb("w2_in", [P, KC, D], at=early)
            h1_in = sb("h1_in", [P, KC, HID], at=early)
            h2_in = sb("h2_in", [P, KC, HID], at=early)
            w3_in = sb("w3_in", [P, HID], at=early)
            scales_in = sb("scales_in", [NSC, P], at=early)
            lo_max = sb("lo_max", [P, 16], at=early)
            lo_flag = sb("lo_flag", [P, 4], at=early)
        x1t_hi, x1t_lo = (sb(f"x1t_{s}", [P, TOK], F32R) for s in ("hi", "lo"))
        act32 = sb("act32", [P, 2, TOK])
        odd_hi, odd_lo = (sb(f"odd_{s}", [P, KC, TOK], F32R) for s in ("hi", "lo"))
        even_hi, even_lo = (sb(f"even_{s}", [P, KC, TOK], F32R) for s in ("hi", "lo"))
        turns_buf = sb("turns_buf", [P, TOK])
        at, tanh_out, yt = turns_buf[:, 0:N], turns_buf, turns_buf

        bank = [ctx.enter_context(nc.psum_tensor(f"bank{n}", [P, 512], F32)) for n in range(8)]
        ff = bank[0:2]
        pj = bank[2]
        sc = bank[3:5]
        pt = bank[5:7]
        acc = bank[7]
        AT_BANK = [pj, ff[0]]
        X1T_BANK, YT_BANK, L4_BANK, XT_BANK = ff[1], ff[1], ff[0], pj
        T_FIRST = [pt[0], pt[1], acc, pj, ff[0], ff[1], pt[0], pt[1]]
        V_FIRST = [acc, pj, ff[0], ff[1]]
        V_BANKS = [pj, pt[(L2_SLOT + 1) % 2]]
        T_BANKS = [pj, pt[(L3_SLOT + 1) % 2]]
        PREP_BANK = [sc[0], sc[1], ff[0], ff[1]]
        SCALES_BANK, FLAG_BANK = ff[0], ff[1]

        (s_wqk, s_wv, s_wf, s_ident, s_prep_mm, s_prep_hi, s_prep_lo, s_lomax, s_flagt, s_flag,
         s_zero, s_scales_mm, s_scales, s_halves, s_held) = (sem(n) for n in (
            "wqk_in", "wv_in", "wf_in", "ident_made", "prep_mm", "prep_hi", "prep_lo", "lomax_made",
            "flag_turned", "flag_made", "zeroed", "scales_mm", "scales_ready", "halves_ready", "held"))
        s_xin, s_res, s_yfree = sem("x_in_landed"), sem("res_landed"), sem("y_stored")
        s_xt_mm, s_xt_hi, s_xt_lo = sem("xt_mm"), sem("xt_hi"), sem("xt_lo")
        s_t_mm, s_t_hi, s_t_lo = sem("t_mm"), sem("t_hi"), sem("t_lo")
        s_v_mm, s_v_hi, s_v_lo = sem("v_mm"), sem("v_hi"), sem("v_lo")
        s_sc, s_max, s_exp, s_inv, s_norm = (sem(n) for n in ("scores", "max", "exp", "inv", "norm"))
        s_pt_mm, s_pt_hi, s_pt_lo, s_pv = (sem(n) for n in ("pt_mm", "pt_hi", "pt_lo", "pv"))
        s_acc, s_at, s_radd = sem("acc_copied"), sem("at_mm"), sem("res_added")
        s_st1, s_mv1, s_st2, s_mv2 = sem("stats1"), sem("mv1"), sem("stats2"), sem("mv2")
        s_ve1, s_rs1, s_x1 = sem("var_eps1"), sem("rstd1"), sem("x1_ready")
        s_x1t_mm, s_x1t_hi, s_x1t_lo = sem("x1t_mm"), sem("x1t_hi"), sem("x1t_lo")
        s_z1, s_z2, s_tanh, s_silu, s_gate, s_l2, s_gelu2, s_l3, s_gelu3 = (sem(n) for n in (
            "z1_mm", "z2_mm", "tanh", "silu", "gate", "l2_mm", "gelu2", "l3_mm", "gelu3"))
        s_1hi, s_1lo, s_2hi, s_2lo, s_3hi, s_3lo = (
            sem(f"l{n}_{s}") for n in (1, 2, 3) for s in ("hi", "lo"))
        s_l4, s_yt, s_yt_mm, s_yadd = sem("l4_mm"), sem("yt_ready"), sem("yt_mm"), sem("y_added")
        s_ve2, s_rs2, s_y = sem("var_eps2"), sem("rstd2"), sem("y_ready")

        block = ctx.enter_context(nc.Block())

        def steps(eng, step):
            step((None, 0), True, True, False, False)
            step((None, 1), True, True, True, False)
            last = (PAIRS - 3) // 2 * 2
            with eng.Fori(2, last - 1, 2) as r:
                step((r, 0), True, True, True, True)
                step((r, 1), True, True, True, True)
            for i in range(last, PAIRS + 2):
                step((None, i), i < PAIRS, i + 1 < PAIRS, i <= PAIRS, True)

        G_ATT = 4
        PREP = [(a_hi[:, 0:4, :], a_lo[:, 0:4, :]), (a_hi[:, 4:8, :], a_lo[:, 4:8, :]),
                (wv_hi[:, 0:512], wv_lo[:, 0:512]), (wv_hi[:, 512:1024], wv_lo[:, 512:1024]),
                (w1_hi[:, :], w1_lo[:, :]), (w2_hi[:, :], w2_lo[:, :])]
        PREP += [(h1_hi[:, c, :], h1_lo[:, c, :]) for c in range(KC)]
        PREP += [(h2_hi[:, c, :], h2_lo[:, c, :]) for c in range(KC)]
        PREP += [(w3_hi[:, :, :], w3_lo[:, :, :])]
        NPREP = len(PREP)
        LATE_V_SLOTS = {1: 2, 2: 3}
        START_SLOT = 3
        PREP_SLOTS = {4: G_ATT, 5: G_ATT + 1, 6: G_ATT + 2}
        FLAG_SLOT = 2

        def prep_of_slot(j, ffn, cur):
            return PREP_SLOTS.get(j) if cur and not ffn else None

        def prep_of_tile(j, k, ffn):
            return G_ATT + 3 + (j == L3_SLOT) * KC + k // 2 if not ffn and k % 2 == 1 else None

        def hold(eng, s, value):
            eng.wait_ge(s, value)
            eng.sem_inc(s_held)

        def prep_bank(g, like):
            b = (PREP_BANK[g] if g < G_ATT else ff[g % 2])[:, :]
            return b.rearrange("p (c n) -> p c n", n=D) if len(like.shape) == 3 else b

        def units(i, j, cur, nxt, ahead):
            if j + ahead < J:
                return [(i, j + ahead)] if cur else []
            return [(plus(i, 1), j + ahead - J)] if nxt else []

        def fills(i, cur, nxt):
            return [(k, i, 4 + k) if k < 4 else (k, plus(i, 1), k - 4)
                    for k in range(2 * KC) if (cur if k < 4 else nxt)]

        def v_cols(n):
            t, half = V_ORDER[n]
            return t, slice(half * TOK, (half + 1) * TOK)

        def v_bank(i, n):
            return V_FIRST[n] if is_first(i) and n < len(V_FIRST) else V_BANKS[n % 2]

        def t_bank(i, h):
            return T_FIRST[h] if is_first(i) else T_BANKS[h % 2]

        def xt_of(i):
            return xt_hi[i[1] % 2], xt_lo[i[1] % 2]

        def alone(f):
            return f[0] is None and f[1] == PAIRS - 1

        def l1_banks(f, c):
            return ((ff[0], ff[1]), (sc[0], sc[1]), (pt[0], pt[1]), (pj, acc))[c] if alone(f) else (ff[0], ff[1])

        def l2_bank(f, o):
            return (ff[0], ff[1], sc[0], sc[1])[o] if alone(f) else ff[o % 2]

        def l3_bank(f, o):
            return (pt[0], pt[1], pj, acc)[o] if alone(f) else ff[o % 2]

        def act_of(f, c):
            return prob[:, c, :, :].rearrange("p t n -> p (t n)") if alone(f) else act32[:, c % 2, :]

        @block.sync
        def _(sp):
            sp.dma_start(x_in[:, :, :], x_rows[0]).then_inc(s_xin, 16)
            sp.dma_start(wq_in[:, :, :], wq.rearrange("(h r) d -> r h d", h=H)).then_inc(s_wqk, 16)
            sp.dma_start(wk_in[:, :, :], wk.rearrange("(h r) d -> r h d", h=H)).then_inc(s_wqk, 16)
            sp.dma_start(wv_in[:, :, :], wv.rearrange("(h p) d -> p h d", h=H)).then_inc(s_wv, 16)
            for n, s in enumerate((w1_s, w2_s, h1_s, h2_s)):
                sp.dma_start(scales_in[n * KC:(n + 1) * KC, :], s.rearrange("(c p) -> c p", p=P)).then_inc(s_wf, 16)
            for n in (4 * KC, 4 * KC + 1):
                sp.dma_start(scales_in[n:n + 1, :], w3_s.rearrange("(a p) -> a p", a=1)).then_inc(s_wf, 16)
            sp.dma_start(w1_in[:, :, :], w1_w.rearrange("(c p) d -> p c d", p=P)).then_inc(s_wf, 16)
            sp.dma_start(w2_in[:, :, :], w2_w.rearrange("(c p) d -> p c d", p=P)).then_inc(s_wf, 16)
            sp.dma_start(h1_in[:, :, :], h1_w.rearrange("(c p) d -> p c d", p=P)).then_inc(s_wf, 16)
            sp.dma_start(h2_in[:, :, :], h2_w.rearrange("(c p) d -> p c d", p=P)).then_inc(s_wf, 16)
            sp.dma_start(w3_in[:, :], w3_w).then_inc(s_wf, 16)
            sp.dma_start(res[:, :, :], x_rows[0]).then_inc(s_res, 16)
            for i in (1, 2):
                sp.wait_ge(s_xt_mm, i)
                sp.dma_start(x_in[:, :, :], x_rows[i]).then_inc(s_xin, 16)

            def step(i, cur, nxt, ffn, tail):
                if ffn and cur:
                    sp.wait_ge(s_x1, count(i, 2, 0))
                    sp.dma_start(res[:, :, :], x_rows[row(i)]).then_inc(s_res, 16)
                if tail:
                    sp.wait_ge(s_y, count(i, 1, -1))
                    sp.dma_start(out_rows[row(plus(i, -2))], y[:, :, :]).then_inc(s_yfree, 16)
                if exists(plus(i, 3)):
                    sp.wait_ge(s_xt_mm, count(i, 1, 3))
                    sp.dma_start(x_in[:, :, :], x_rows[row(plus(i, 3))]).then_inc(s_xin, 16)

            steps(sp, step)
            sp.wait_ge(s_yfree, 16 * PAIRS)

        @block.gpsimd
        def _(pool):
            nc.gpsimd.memset(ident[:, :], 0.0).then_inc(s_zero, 1)
            nc.gpsimd.memset(minus_half[:, :], -0.5).then_inc(s_zero, 1)
            pool.wait_ge(s_zero, 1)
            nc.gpsimd.affine_select(out=ident[:, :], in_=ident[:, :], compare_op=ALU.not_equal, fill=1.0,
                                    base=0, pattern=[[-1, P]], channel_multiplier=1).then_inc(s_ident, 1)

            def norm(i, j):
                pool.wait_ge(s_inv, count(i, J, j + 1))
                nc.gpsimd.tensor_tensor(prob[:, j % RING, :, :], prob[:, j % RING, :, :],
                                        inv_total[:, j % RING, :].unsqueeze(2).to_broadcast([P, NT, N]),
                                        ALU.mult).then_inc(s_norm, 1)

            def lo_part(f, c, hi, lo, s_in, s_lo):
                pool.wait_ge(s_in, count(f, KC, c + 1))
                nc.gpsimd.tensor_tensor(lo[:, c, :], act_of(f, c), hi[:, c, :].bitcast(F32),
                                        ALU.subtract).then_inc(s_lo, 1)

            def rstd(f, part, parts, mv, var_eps, out_rstd, s_mv, s_ve, s_rs):
                n = TT // parts
                t = slice(part * n, (part + 1) * n)
                hold(pool, s_mv, count(f, TT, (part + 1) * n))
                nc.gpsimd.tensor_scalar(var_eps[:, t], mv[:, t, 1], EPS, None, ALU.add).then_inc(s_ve, 1)
                pool.wait_ge(s_ve, count(f, parts, part + 1))
                nc.gpsimd.tensor_tensor(out_rstd[:, t], var_eps[:, t], minus_half[:, t], ALU.pow).then_inc(s_rs, 1)

            def norm2(g, t):
                last = nc.gpsimd.tensor_scalar(y[:, t, :], y[:, t, :], mv2[:, t, 0:1], rstd2[:, t:t + 1],
                                               ALU.subtract, ALU.mult)
                if t == TT - 1:
                    last.then_inc(s_y, 1)

            for j in range(LEAD - 1):
                norm((None, 0), j)

            def step(i, cur, nxt, ffn, tail):
                f, g = plus(i, -1), plus(i, -2)
                for j in range(J):
                    for pair, u in units(i, j, cur, nxt, LEAD - 1):
                        norm(pair, u)
                    if ffn and j in L1_SLOTS:
                        lo_part(f, j - L1_SLOTS[0], odd_hi, odd_lo, s_1hi, s_1lo)
                    if tail and j == NORM2_SLOT:
                        if ffn and not alone(f):
                            lo_part(f, 0, even_hi, even_lo, s_2hi, s_2lo)
                        rstd(g, 0, 1, mv2, var_eps2, rstd2, s_mv2, s_ve2, s_rs2)
                        hold(pool, s_rs2, count(g, 1, 1))
                        for c in range(1, KC):
                            if ffn and not alone(f):
                                lo_part(f, c, even_hi, even_lo, s_2hi, s_2lo)
                            if c < 3 and not alone(g):
                                norm2(g, c - 1)
                    if tail and not alone(g) and j in (NORM2_SLOT + 1, NORM2_SLOT + 2):
                        norm2(g, j - NORM2_SLOT + 1)
                    if cur and j == STATS1_SLOT + 1:
                        rstd(i, 0, 2, mv1, var_eps1, rstd1, s_mv1, s_ve1, s_rs1)
                    if not ffn:
                        continue
                    if j == AT1_SLOT:
                        rstd(f, 1, 2, mv1, var_eps1, rstd1, s_mv1, s_ve1, s_rs1)
                    for c in range(KC):
                        if j == L2_SLOT and not tail:
                            lo_part(f, c, even_hi, even_lo, s_2hi, s_2lo)
                        if j == L3_SLOT and not alone(f):
                            lo_part(f, c, odd_hi, odd_lo, s_3hi, s_3lo)

            steps(pool, step)

        @block.scalar
        def _(act):
            def copy(dst, src):
                return nc.scalar.activation(dst, src, ACT.Copy)

            def prep(g):
                act.wait_ge(s_prep_mm, g + 1)
                copy(PREP[g][0], prep_bank(g, PREP[g][0])).then_inc(s_prep_hi, 1)

            def xt_part(i):
                act.wait_ge(s_xt_mm, count(i, 1, 1))
                copy(xt_of(i)[0][:, :], XT_BANK[:, :]).then_inc(s_xt_hi, 1)

            def t_part(i, h):
                act.wait_ge(s_t_mm, count(i, H, h + 1))
                copy(t_hi[:, h, :], t_bank(i, h)[:, :]).then_inc(s_t_hi, 1)

            def v_part(i, n):
                t, cols = v_cols(n)
                act.wait_ge(s_v_mm, count(i, VT, n + 1))
                copy(v_hi[:, t, cols], v_bank(i, n)[:, :]).then_inc(s_v_hi, 1)

            def acc_copy(i, b):
                act.wait_ge(s_pv, count(i, J, (b + 1) * H))
                if b == 0:
                    need(act, s_silu, count(i, KC, 0))
                else:
                    need(act, s_yt_mm, count(i, 1, 0))
                copy(at, acc[:, b * N:(b + 1) * N]).then_inc(s_acc, 1)

            def exp(i, j):
                act.wait_ge(s_max, count(i, J, j + 1))
                need(act, s_pt_mm, count(i, J, j - RING + 1))
                for nt in range(NT):
                    last = nc.scalar.activation(prob[:, j % RING, nt, :], sc[j % 2][:, nt * N:(nt + 1) * N],
                                                ACT.Exp, bias=neg_max[:, j % RING, nt:nt + 1],
                                                accum_out=total[:, j % RING, nt:nt + 1])
                last.then_inc(s_exp, 1)

            def pt_part(i, j):
                act.wait_ge(s_pt_mm, count(i, J, j + 1))
                need(act, s_pv, count(i, J, j - RING + 1))
                copy(pt_hi[:, j % RING, :, :], pt[j % 2].rearrange("p (t n) -> p t n", n=N)).then_inc(s_pt_hi, 1)

            def tanh(f, c):
                act.wait_ge(s_z1, count(f, KC, c + 1))
                if c == 0:
                    act.wait_ge(s_at, count(f, 2, 2))
                else:
                    act.wait_ge(s_silu, count(f, KC, c))
                nc.scalar.activation(tanh_out[:, :], l1_banks(f, c)[0][:, :], ACT.Tanh,
                                     scale=half_s1[:, c:c + 1]).then_inc(s_tanh, 1)

            def l1_hi(f, c):
                act.wait_ge(s_gate, count(f, KC, c + 1))
                copy(odd_hi[:, c, :], act_of(f, c)).then_inc(s_1hi, 1)

            def gelu(f, c, n_scale, bank_of, s_mm, s_prior_lo, n_prior, s_out):
                act.wait_ge(s_mm, count(f, KC, c + 1))
                if not alone(f):
                    act.wait_ge(s_prior_lo, count(f, KC, n_prior))
                nc.scalar.activation(act_of(f, c), bank_of(f, c)[:, :], ACT.Gelu,
                                     scale=scales[:, n_scale * KC + c:n_scale * KC + c + 1]).then_inc(s_out, 1)

            xt_part((None, 0))
            prep(0)
            prep(1)
            prep(2)
            prep(3)
            first = (None, 0)
            for h in range(6):
                t_part(first, h)
            exp(first, 0)
            t_part(first, 6)
            exp(first, 1)
            t_part(first, 7)
            v_part(first, 0)
            v_part(first, 1)
            exp(first, 2)

            def step(i, cur, nxt, ffn, tail):
                f, i1, i2 = plus(i, -1), plus(i, 1), plus(i, 2)
                for j in range(J):
                    g = prep_of_slot(j - 1, ffn, cur)
                    if g is not None:
                        prep(g)
                    after_burst = j - 1 in (L2_SLOT, L3_SLOT)
                    if cur and not after_burst:
                        pt_part(i, j)
                    if ffn and alone(f) and j in L1_SLOTS:
                        tanh(f, j - L1_SLOTS[0])
                    if ffn and j - 1 in L1_SLOTS:
                        l1_hi(f, j - 1 - L1_SLOTS[0])
                    if ffn and not alone(f) and j in L1_SLOTS:
                        tanh(f, j - L1_SLOTS[0])
                    if ffn and j == LAG - 1:
                        acc_copy(f, 1)
                    if ffn and j == X1T_SLOT:
                        act.wait_ge(s_x1t_mm, count(f, 1, 1))
                        copy(x1t_hi[:, :], X1T_BANK[:, :]).then_inc(s_x1t_hi, 1)
                    for pair, u in units(i, j, cur, nxt, LEAD):
                        if j not in (L2_SLOT, L3_SLOT):
                            exp(pair, u)
                    if cur and after_burst:
                        pt_part(i, j)
                    if cur and not ffn and j in LATE_V_SLOTS:
                        v_part(i, LATE_V_SLOTS[j])
                    if cur and not ffn and j == START_SLOT:
                        xt_part(i1)
                        act.wait_ge(s_scales_mm, 1)
                        copy(scales[:, :], SCALES_BANK[:, 0:NSC]).then_inc(s_scales, 1)
                    if j == L2_SLOT:
                        tiles = fills(i, cur, nxt)
                        for c in range(KC):
                            for k, pair, n in tiles:
                                if c == 0 and k == (1 if ffn else 2):
                                    for unit in units(i, j, cur, nxt, LEAD):
                                        exp(*unit)
                                    acc_copy(i, 0)
                                if k in TILES_BEFORE[c]:
                                    v_part(pair, n)
                                    if prep_of_tile(j, k, ffn):
                                        prep(prep_of_tile(j, k, ffn))
                            if ffn:
                                gelu(f, c, 2, l2_bank, s_l2, *((s_1lo, KC - 1 + c) if c < 2 else (s_2lo, c - 1)), s_gelu2)
                    if j == L3_SLOT:
                        for c in range(KC):
                            for h in TILES_BEFORE[c] if nxt else ():
                                if h == (1 if ffn else 2):
                                    exp(i, j + LEAD)
                                t_part(i1, h)
                                if prep_of_tile(j, h, ffn):
                                    prep(prep_of_tile(j, h, ffn))
                            if cur and not nxt and c == 0:
                                exp(i, j + LEAD)
                            if ffn:
                                gelu(f, c, 3, l3_bank, s_l3, *((s_2lo, KC - 1 + c) if c < 2 else (s_3lo, c - 1)), s_gelu3)
                    if cur and exists(i2) and j == XT_SLOT:
                        xt_part(i2)
                    if ffn and j == L4_SLOT:
                        act.wait_ge(s_l4, count(f, 1, 1))
                        if cur:
                            act.wait_ge(s_at, count(i, 2, 1))
                        nc.scalar.activation(yt[:, :], L4_BANK[:, :], ACT.Copy,
                                             scale=scales[:, 4 * KC:4 * KC + 1]).then_inc(s_yt, 1)

            steps(act, step)

        @block.vector
        def _(dve):
            def minus(dst, src, hi):
                return nc.vector.tensor_tensor(dst, src, hi.bitcast(F32), ALU.subtract)

            def prep(g):
                hi, lo = PREP[g]
                dve.wait_ge(s_prep_hi, g + 1)
                minus(lo, prep_bank(g, lo), hi).then_inc(s_prep_lo, 1)

            def largest_lo(g):
                lo = PREP[g][1]
                dve.wait_ge(s_prep_lo, g + 1)
                nc.vector.tensor_reduce(lo_max[:, g - G_ATT:g - G_ATT + 1], lo.bitcast(F32),
                                        AX.X if len(lo.shape) == 2 else AX.XY,
                                        ALU.max, apply_absolute_value=True).then_inc(s_lomax, 1)

            def xt_part(i):
                hi, lo = xt_of(i)
                dve.wait_ge(s_xt_hi, count(i, 1, 1))
                minus(lo[:, :], XT_BANK[:, :], hi[:, :]).then_inc(s_xt_lo, 1)

            def t_part(i, h):
                dve.wait_ge(s_t_hi, count(i, H, h + 1))
                minus(t_lo[:, h, :], t_bank(i, h)[:, :], t_hi[:, h, :]).then_inc(s_t_lo, 1)

            def v_part(i, n):
                t, cols = v_cols(n)
                dve.wait_ge(s_v_hi, count(i, VT, n + 1))
                minus(v_lo[:, t, cols], v_bank(i, n)[:, :], v_hi[:, t, cols]).then_inc(s_v_lo, 1)

            def row_max(i, j):
                dve.wait_ge(s_sc, count(i, J, j + 1))
                nc.vector.tensor_reduce(neg_max[:, j % RING, :], sc[j % 2].rearrange("p (t m) -> p t m", m=N),
                                        AX.X, ALU.max, negate=True).then_inc(s_max, 1)

            def inverse(i, j):
                dve.wait_ge(s_exp, count(i, J, j + 1))
                nc.vector.reciprocal(inv_total[:, j % RING, :], total[:, j % RING, :]).then_inc(s_inv, 1)

            def res_add(i, b):
                dve.wait_ge(s_at, count(i, 2, b + 1))
                if b == 0:
                    dve.wait_ge(s_res, count(i, 16, 16))
                half = res[:, NT * b:NT * (b + 1), :]
                nc.vector.tensor_tensor(half, AT_BANK[b][:, 0:N].rearrange("p (t d) -> p t d", d=D), half,
                                        ALU.add).then_inc(s_radd, 1)

            def stats(i, src, tiles, stat, mv, s_src, n_src, s_st, s_mv):
                dve.wait_ge(s_src, n_src)
                for t in tiles:
                    nc.vector.bn_stats(stat[:, t, :], src[:, t, :]).then_inc(s_st, 1)
                for t in tiles:
                    hold(dve, s_st, count(i, TT, t + 1))
                    nc.vector.bn_aggr(mv[:, t, :], stat[:, t, :]).then_inc(s_mv, 1)

            def stats_res(i, b):
                stats(i, res, range(NT * b, NT * (b + 1)), stats1, mv1, s_radd, count(i, 2, b + 1), s_st1, s_mv1)

            def stats_y(g):
                stats(g, y, range(TT), stats2, mv2, s_yadd, count(g, 1, 1), s_st2, s_mv2)
                if alone(g):
                    hold(dve, s_rs2, count(g, 1, 1))
                    for t in range(TT):
                        last = nc.vector.tensor_scalar(y[:, t, :], y[:, t, :], mv2[:, t, 0:1], rstd2[:, t:t + 1],
                                                       ALU.subtract, ALU.mult)
                    last.then_inc(s_y, 1)

            def norm1(f, b):
                dve.wait_ge(s_rs1, count(f, 2, b + 1))
                need(dve, s_yadd, count(f, 1, 0))
                for t in range(NT * b, NT * (b + 1)):
                    last = nc.vector.tensor_scalar(x1[:, t, :], res[:, t, :], mv1[:, t, 0:1],
                                                   rstd1[:, t:t + 1], ALU.subtract, ALU.mult)
                last.then_inc(s_x1, 1)

            def gate(f, c):
                a32 = act_of(f, c)
                dve.wait_ge(s_tanh, count(f, KC, c + 1))
                z1, z2 = l1_banks(f, c)
                if alone(f):
                    pass
                elif c < 2:
                    need(dve, s_3lo, count(f, KC, c - 1))
                else:
                    dve.wait_ge(s_1lo, count(f, KC, c - 1))
                nc.vector.scalar_tensor_tensor(out=a32, in0=tanh_out[:, :], scalar=1.0,
                                               in1=z1[:, :], op0=ALU.add, op1=ALU.mult).then_inc(s_silu, 1)
                dve.wait_ge(s_silu, count(f, KC, c + 1))
                dve.wait_ge(s_z2, count(f, KC, c + 1))
                nc.vector.scalar_tensor_tensor(out=a32, in0=z2[:, :], scalar=half_s12[:, c:c + 1],
                                               in1=a32, op0=ALU.mult, op1=ALU.mult).then_inc(s_gate, 1)

            def hi_part(f, c, hi, lo, s_in, s_hi, s_lo):
                dve.wait_ge(s_in, count(f, KC, c + 1))
                nc.vector.tensor_copy(hi[:, c, :], act_of(f, c)).then_inc(s_hi, 1)
                if alone(f):
                    dve.wait_ge(s_hi, count(f, KC, c + 1))
                    minus(lo[:, c, :], act_of(f, c), hi[:, c, :]).then_inc(s_lo, 1)

            first = (None, 0)
            xt_part(first)
            prep(0)
            prep(1)
            prep(2)
            prep(3)
            for h in range(6):
                t_part(first, h)
            row_max(first, 0)
            row_max(first, 1)
            t_part(first, 6)
            inverse(first, 0)
            t_part(first, 7)
            row_max(first, 2)
            inverse(first, 1)
            v_part(first, 0)
            v_part(first, 1)

            def flag_by_partition():
                dve.wait_ge(s_lomax, NPREP - G_ATT)
                nc.vector.tensor_reduce(lo_max[:, 15:16], lo_max[:, 0:NPREP - G_ATT], AX.X, ALU.max).then_inc(s_lomax, 1)

            def flag():
                dve.wait_ge(s_flagt, 1)
                nc.vector.tensor_reduce(lo_flag[0:1, 0:1], FLAG_BANK[0:1, 0:P], AX.X, ALU.max).then_inc(s_flag, 1)

            def halves():
                dve.wait_ge(s_scales, 1)
                nc.vector.tensor_scalar(half_s1[:, :], scales[:, 0:KC], 0.5, None, ALU.mult).then_inc(s_halves, 1)
                dve.wait_ge(s_halves, 1)
                nc.vector.tensor_tensor(half_s12[:, :], half_s1[:, :], scales[:, KC:2 * KC], ALU.mult).then_inc(s_halves, 1)
                dve.wait_ge(s_halves, 2)

            def step(i, cur, nxt, ffn, tail):
                f, g, i1, i2 = (plus(i, n) for n in (-1, -2, 1, 2))
                for j in range(J):
                    for pair, u in units(i, j, cur, nxt, LEAD):
                        row_max(pair, u)
                    for pair, u in units(i, j, cur, nxt, LEAD - 1):
                        inverse(pair, u)
                    group = prep_of_slot(j - 1, ffn, cur)
                    if group is not None:
                        prep(group)
                    if ffn and j in NORM1_SLOTS:
                        norm1(f, NORM1_SLOTS.index(j))
                    if ffn and j == AT1_SLOT:
                        res_add(f, 1)
                        stats_res(f, 1)
                    if cur:
                        dve.wait_ge(s_pt_hi, count(i, J, j + 1))
                        minus(pt_lo[:, j % RING, :, :], pt[j % 2].rearrange("p (t n) -> p t n", n=N),
                              pt_hi[:, j % RING, :, :]).then_inc(s_pt_lo, 1)
                    if group is not None:
                        largest_lo(group)
                    if ffn and j == X1T_SLOT:
                        dve.wait_ge(s_x1t_hi, count(f, 1, 1))
                        minus(x1t_lo[:, :], X1T_BANK[:, :], x1t_hi[:, :]).then_inc(s_x1t_lo, 1)
                    if ffn and j in L1_SLOTS:
                        gate(f, j - L1_SLOTS[0])
                    if j == L2_SLOT:
                        tiles = fills(i, cur, nxt)
                        for c in range(KC):
                            for k, pair, n in tiles:
                                if k in TILES_BEFORE[c]:
                                    v_part(pair, n)
                                    if prep_of_tile(j, k, ffn):
                                        prep(prep_of_tile(j, k, ffn))
                                        largest_lo(prep_of_tile(j, k, ffn))
                                if tail and c == 0 and k == 1:
                                    stats_y(g)
                            if tail and not cur and c == 0:
                                stats_y(g)
                            if ffn:
                                hi_part(f, c, even_hi, even_lo, s_gelu2, s_2hi, s_2lo)
                    if cur and j == AT0_SLOT:
                        res_add(i, 0)
                    if j == L3_SLOT:
                        for c in range(KC):
                            for h in TILES_BEFORE[c] if nxt else ():
                                t_part(i1, h)
                                if prep_of_tile(j, h, ffn):
                                    prep(prep_of_tile(j, h, ffn))
                                    largest_lo(prep_of_tile(j, h, ffn))
                            if ffn:
                                hi_part(f, c, odd_hi, odd_lo, s_gelu3, s_3hi, s_3lo)
                    if cur and not ffn and j in LATE_V_SLOTS:
                        v_part(i, LATE_V_SLOTS[j])
                    if cur and not ffn and j == START_SLOT:
                        xt_part(i1)
                        halves()
                    if cur and not ffn and j == J - 2:
                        flag_by_partition()
                    if ffn and not tail and j == FLAG_SLOT + 1:
                        flag()
                    if cur and exists(i2) and j == XT_SLOT:
                        xt_part(i2)
                    if cur and j == STATS1_SLOT:
                        stats_res(i, 0)
                    if ffn and j == YT_SLOT:
                        dve.wait_ge(s_yt_mm, count(f, 1, 1))
                        need(dve, s_yfree, count(f, 16, 0))
                        nc.vector.tensor_tensor(y[:, :, :], YT_BANK.rearrange("p (t d) -> p t d", d=D),
                                                x1[:, :, :], ALU.add).then_inc(s_yadd, 1)

            steps(dve, step)

        @block.tensor
        def _(pe):
            mm, turn = nc.tensor.matmul, nc.tensor.transpose
            any_lo = []

            def three(dst, w_hi, w_lo, m_hi, m_lo, start, stop):
                mm(dst, w_hi, m_hi, start=start, stop=False)
                mm(dst, w_hi, m_lo, start=False, stop=False)
                return mm(dst, w_lo, m_hi, start=False, stop=stop)

            def turns(dst, blocks, s_out):
                for n, b in enumerate(blocks):
                    last = turn(dst[:, n * P:(n + 1) * P], b, ident[:, :])
                last.then_inc(s_out, 1)

            def turn_x(i):
                pe.wait_ge(s_xin, count(i, 16, 16))
                turns(XT_BANK, [x_in[:, t, :] for t in range(TT)], s_xt_mm)

            def project_t(i, h):
                hi, lo = xt_of(i)
                three(t_bank(i, h)[:, :], a_hi[:, h, :], a_lo[:, h, :], hi[:, :], lo[:, :],
                      True, True).then_inc(s_t_mm, 1)

            def project_v(i, n):
                hi, lo = xt_of(i)
                t, cols = v_cols(n)
                rows = slice(t * P, (t + 1) * P)
                three(v_bank(i, n)[:, :], hi[:, rows], lo[:, rows], wv_hi[:, cols], wv_lo[:, cols],
                      True, True).then_inc(s_v_mm, 1)

            def scores(i, j):
                b, h = j // H, j % H
                hi, lo = xt_of(i)
                if j < H:
                    pe.wait_ge(s_t_lo, count(i, H, h + 1))
                need(pe, s_exp, count(i, J, j - 1))
                for nt in range(NT):
                    q = slice(b * N + nt * P, b * N + (nt + 1) * P)
                    m = slice(b * N, (b + 1) * N)
                    last = three(sc[j % 2][:, nt * N:(nt + 1) * N], t_hi[:, h, q], t_lo[:, h, q],
                                 hi[:, m], lo[:, m], True, True)
                last.then_inc(s_sc, 1)

            def turn_prob(i, j):
                pe.wait_ge(s_norm, count(i, J, j + 1))
                if is_first(i) and j == 0:
                    pe.wait_ge(s_t_lo, 7)
                if is_first(i) and j == 1:
                    pe.wait_ge(s_t_lo, 8)
                if j == L2_SLOT + 1:
                    pe.wait_ge(s_v_lo, count(i, VT, VT + 4 if exists(plus(i, 1)) else VT))
                if j == L3_SLOT + 1 and exists(plus(i, 1)):
                    pe.wait_ge(s_t_lo, count(plus(i, 1), H, H))
                need(pe, s_pt_lo, count(i, J, j - 1))
                turns(pt[j % 2], [prob[:, j % RING, nt, mt * P:(mt + 1) * P]
                                  for mt in range(NT) for nt in range(NT)], s_pt_mm)

            def times_v(i, j):
                b, h = j // H, j % H
                pe.wait_ge(s_pt_lo, count(i, J, j + 1))
                if j in V_OF_UNIT:
                    pe.wait_ge(s_v_lo, count(i, VT, V_OF_UNIT[j]))
                if h == 0:
                    need(pe, s_acc, count(i, 2, b))
                for mt in range(NT):
                    v = slice(h * D, (h + 1) * D)
                    last = three(acc[:, b * N:(b + 1) * N], v_hi[:, b * NT + mt, v], v_lo[:, b * NT + mt, v],
                                 pt_hi[:, j % RING, mt, :], pt_lo[:, j % RING, mt, :],
                                 h == 0 and mt == 0, h == H - 1 and mt == NT - 1)
                last.then_inc(s_pv, 1)

            def turn_attention(i, b):
                pe.wait_ge(s_acc, count(i, 2, b + 1))
                turns(AT_BANK[b], [at[:, t * P:(t + 1) * P] for t in range(NT)], s_at)

            def layer(dst, w_hi, w_lo, m_hi, m_lo, with_lo, s_parts=None, first=0, between=None):
                n = len(w_hi)
                for c in range(n):
                    if between is not None and c == n // 2:
                        between()
                    if s_parts is not None:
                        pe.wait_ge(s_parts, first + c)
                    mm(dst, w_hi[c], m_hi[c], start=(c == 0), stop=False)
                    last = mm(dst, w_hi[c], m_lo[c], start=False, stop=(c == n - 1 and not with_lo))
                    if with_lo:
                        last = mm(dst, w_lo[c], m_hi[c], start=False, stop=(c == n - 1))
                return last

            def either(emit):
                with pe.If(any_lo[0]):
                    emit(True)
                with pe.Else():
                    emit(False)

            def layer1(f, o, with_lo):
                cols = slice(o * P, (o + 1) * P)
                if o == 0:
                    pe.wait_ge(s_x1t_lo, count(f, 1, 1))
                    pe.wait_ge(s_radd, count(f, 2, 2))
                z1, z2 = l1_banks(f, o)
                for b, hi, lo, s_read, s_out in ((z1, w1_hi, w1_lo, s_silu, s_z1), (z2, w2_hi, w2_lo, s_gate, s_z2)):
                    if o > 0 and not alone(f):
                        pe.wait_ge(s_read, count(f, KC, o))
                    layer(b[:, :], [hi[:, cols]], [lo[:, cols]], [x1t_hi[:, :]], [x1t_lo[:, :]],
                          with_lo).then_inc(s_out, 1)

            def layer23(f, between, w_hi, w_lo, m_hi, m_lo, prior, s_parts, s_gelu, s_out, with_lo):
                for o in range(KC):
                    cols = slice(o * P, (o + 1) * P)
                    between(2 * o)
                    if o < 2:
                        pe.wait_ge(prior[o][0], count(f, KC, prior[o][1]))
                    else:
                        pe.wait_ge(s_gelu, count(f, KC, o - 1))
                    layer(ff[o % 2][:, :], [w_hi[:, c, cols] for c in range(KC)],
                          [w_lo[:, c, cols] for c in range(KC)], [m_hi[:, c, :] for c in range(KC)],
                          [m_lo[:, c, :] for c in range(KC)], with_lo,
                          s_parts if o == 0 else None, count(f, KC, 1),
                          lambda: between(2 * o + 1)).then_inc(s_out, 1)

            def layer_wide(f, bank_of, w_hi, w_lo, m_hi, m_lo, s_parts, s_out, with_lo):
                for c in range(KC):
                    pe.wait_ge(s_parts, count(f, KC, c + 1))
                    for o in range(KC):
                        if c == 0 and o == 2:
                            pe.wait_ge(s_gate, count(f, KC, 2))
                        cols = slice(o * P, (o + 1) * P)
                        dst = bank_of(f, o)[:, :]
                        mm(dst, w_hi[:, c, cols], m_hi[:, c, :], start=(c == 0), stop=False)
                        last = mm(dst, w_hi[:, c, cols], m_lo[:, c, :], start=False, stop=(c == KC - 1 and not with_lo))
                        if with_lo:
                            last = mm(dst, w_lo[:, c, cols], m_hi[:, c, :], start=False, stop=(c == KC - 1))
                        if c == KC - 1:
                            last.then_inc(s_out, 1)

            def layer4(f, with_lo):
                if not alone(f):
                    pe.wait_ge(s_gelu3, count(f, KC, 3))
                layer(L4_BANK[:, :], [w3_hi[:, c, :] for c in range(KC)], [w3_lo[:, c, :] for c in range(KC)],
                      [odd_hi[:, c, :] for c in range(KC)], [odd_lo[:, c, :] for c in range(KC)], with_lo,
                      s_3lo, count(f, KC, 1)).then_inc(s_l4, 1)

            first = (None, 0)
            pe.wait_ge(s_ident, 1)
            turn_x(first)
            pe.wait_ge(s_wqk, 32)
            for g in range(2):
                for h in range(4):
                    last = mm(PREP_BANK[g][:, h * D:(h + 1) * D], wq_in[:, 4 * g + h, :], wk_in[:, 4 * g + h, :],
                              start=True, stop=True)
                last.then_inc(s_prep_mm, 1)
            pe.wait_ge(s_wv, 16)
            for g in range(2):
                turns(PREP_BANK[2 + g], [wv_in[:, 4 * g + h, :] for h in range(4)], s_prep_mm)
            blocks = [[w1_in[:, c, :] for c in range(KC)], [w2_in[:, c, :] for c in range(KC)]]
            for w in (h1_in, h2_in):
                blocks += [[w[:, o, c * P:(c + 1) * P] for o in range(KC)] for c in range(KC)]
            blocks += [[w3_in[:, c * P:(c + 1) * P] for c in range(KC)]]

            pe.wait_ge(s_prep_lo, 2)
            pe.wait_ge(s_xt_lo, 1)
            for h in range(6):
                if h == 4:
                    pe.wait_ge(s_prep_lo, G_ATT)
                project_t(first, h)
            scores(first, 0)
            scores(first, 1)
            project_t(first, 6)
            project_t(first, 7)
            scores(first, 2)
            for n in range(2):
                pe.wait_ge(s_t_lo, 3 + n)
                project_v(first, n)

            def prep(g):
                if g < G_ATT + 2:
                    pe.wait_ge(s_scales, 1)
                    pe.wait_ge(s_v_lo, 4)
                else:
                    pe.wait_ge(s_prep_lo, g - 1)
                turns(prep_bank(g, bank[0][:, :]), blocks[g - G_ATT], s_prep_mm)

            def start():
                pe.wait_ge(s_v_lo, 2)
                turn_x((None, 1))
                pe.wait_ge(s_v_lo, 3)
                pe.wait_ge(s_wf, 16 * 11)
                turn(SCALES_BANK[:, 0:NSC], scales_in[:, :], ident[0:NSC, 0:NSC]).then_inc(s_scales_mm, 1)

            def flag():
                pe.wait_ge(s_lomax, NPREP - G_ATT + 1)
                pe.wait_ge(s_prep_lo, NPREP)
                turn(FLAG_BANK[0:1, 0:P], lo_max[:, 15:16], ident[:, :]).then_inc(s_flagt, 1)

            def step(i, cur, nxt, ffn, tail):
                f, i1, i2 = plus(i, -1), plus(i, 1), plus(i, 2)
                for j in range(J):
                    for pair, u in units(i, j, cur, nxt, LEAD):
                        scores(pair, u)
                    if cur:
                        turn_prob(i, j)
                    if ffn and j == AT1_SLOT:
                        need(pe, s_yt, count(f, 1, 0))
                        turn_attention(f, 1)
                    if j >= LAG and cur:
                        times_v(i, j - LAG)
                    if j < LAG and ffn:
                        times_v(f, j - LAG + J)

                    g = prep_of_slot(j, ffn, cur)
                    if g is not None:
                        prep(g)
                    if cur and not ffn and j in LATE_V_SLOTS:
                        pe.wait_ge(s_t_lo, 3 + LATE_V_SLOTS[j])
                        project_v(i, LATE_V_SLOTS[j])
                    if cur and not ffn and j == START_SLOT:
                        start()
                    if ffn and not tail and j == FLAG_SLOT:
                        flag()
                    if ffn and not tail and j == FLAG_SLOT + 2:
                        load_flag()
                    if ffn and j == X1T_SLOT:
                        pe.wait_ge(s_x1, count(f, 2, 2))
                        need(pe, s_yadd, count(f, 1, 0))
                        turns(X1T_BANK, [x1[:, t, :] for t in range(TT)], s_x1t_mm)
                    if ffn and j in L1_SLOTS:
                        either(lambda w: layer1(f, j - L1_SLOTS[0], w))
                    if j == L2_SLOT:
                        def values(place):
                            for k, pair, n in fills(i, cur, nxt):
                                if k == place:
                                    if k == 0 and nxt:
                                        pe.wait_ge(s_xt_lo, count(i1, 1, 1))
                                    elif k == 0:
                                        pe.wait_ge(s_t_lo, count(i, H, H - 1))
                                    elif k == 1:
                                        pe.wait_ge(s_pt_lo, count(i, J, j))
                                    else:
                                        pe.wait_ge(s_v_lo, count(i, VT, k + 3))
                                    project_v(pair, n)

                        if ffn and alone(f):
                            either(lambda w: layer_wide(f, l2_bank, h1_hi, h1_lo, odd_hi, odd_lo, s_1lo, s_l2, w))
                        elif ffn:
                            either(lambda w: layer23(f, values, h1_hi, h1_lo, odd_hi, odd_lo, ((s_silu, KC), (s_gate, KC)),
                                                     s_1lo, s_gelu2, s_l2, w))
                        else:
                            for k in range(2 * KC):
                                values(k)
                                if cur and prep_of_tile(j, k, ffn):
                                    prep(prep_of_tile(j, k, ffn))
                    if cur and j == AT0_SLOT:
                        pe.wait_ge(s_v_lo, count(i, VT, VT + 3 if nxt else VT - 1))
                        turn_attention(i, 0)
                    if j == L3_SLOT:
                        def heads(h):
                            if nxt:
                                if h == 0:
                                    pe.wait_ge(s_radd, count(i, 2, 1))
                                elif h == 1:
                                    pe.wait_ge(s_pt_lo, count(i, J, j))
                                else:
                                    pe.wait_ge(s_t_lo, count(i1, H, h - 1))
                                project_t(i1, h)

                        if ffn and alone(f):
                            either(lambda w: layer_wide(f, l3_bank, h2_hi, h2_lo, even_hi, even_lo, s_2lo, s_l3, w))
                        elif ffn:
                            either(lambda w: layer23(f, heads, h2_hi, h2_lo, even_hi, even_lo,
                                                     ((s_gelu2, KC - 1), (s_gelu2, KC)),
                                                     s_2lo, s_gelu3, s_l3, w))
                        else:
                            for h in range(2 * KC):
                                heads(h)
                                if cur and prep_of_tile(j, h, ffn):
                                    prep(prep_of_tile(j, h, ffn))
                    if cur and exists(i2) and j == XT_SLOT:
                        pe.wait_ge(s_t_lo, count(i1, H, H - 1))
                        turn_x(i2)
                    if ffn and j == L4_SLOT:
                        either(lambda w: layer4(f, w))
                    if ffn and j == YT_SLOT:
                        pe.wait_ge(s_yt, count(f, 1, 1))
                        turns(YT_BANK, [yt[:, t * P:(t + 1) * P] for t in range(TT)], s_yt_mm)

            def load_flag():
                pe.wait_ge(s_flag, 1)
                any_lo.append(pe.value_load(lo_flag[0:1, 0:1].bitcast(I32)))

            steps(pe, step)


_INS = ["L0_attn_x", "L0_attn_Wq", "L0_attn_Wk", "L0_attn_Wv", "L0_ffn_w1_w", "L0_ffn_w1_s", "L0_ffn_w2_w",
        "L0_ffn_w2_s", "L0_ffn_h1_w", "L0_ffn_h1_s", "L0_ffn_h2_w", "L0_ffn_h2_s", "L0_ffn_w3_w", "L0_ffn_w3_s"]


def kernel(**inputs):
    import numpy as np
    import concourse.bacc as bacc
    from concourse.bass_utils import run_bass_kernel_spmd

    nc = bacc.Bacc("TRN2", target_bir_lowering=False, num_devices=1)
    arrays, args = {}, []
    for name in _INS:
        a = np.ascontiguousarray(inputs[name])
        arrays[f"in_{name}"] = a
        args.append(nc.dram_tensor(f"in_{name}", a.shape, mybir.dt.from_np(a.dtype), kind="ExternalInput").ap())
    shape = arrays["in_L0_attn_x"].shape
    args.append(nc.dram_tensor("out_x", shape, F32, kind="ExternalOutput").ap())
    layer_kernel(nc, *args)
    r = run_bass_kernel_spmd(nc, [arrays], core_ids=[0])
    return r.results[0]["out_x"]
```
